# Optimizing a Trainium2 kernel written in Bass

```python
import numpy as np
import jax
import jax.numpy as jnp

def _softmax(x, axis=-1):
    return jax.nn.softmax(x, axis=axis)

def _gelu(x):
    return jax.nn.gelu(x, approximate=True)

def _silu(x):
    return jax.nn.silu(x)

def _sigmoid(x):
    return jax.nn.sigmoid(x)

def _layernorm(x, axis=-1, eps=1e-05):
    m = jnp.mean(x, axis=axis, keepdims=True)
    v = jnp.var(x, axis=axis, keepdims=True)
    return (x - m) / jnp.sqrt(v + eps)

def _scatter_add(tgt, idx, src, axis=0):
    return tgt.at[idx].add(src)

def _segment_sum(src, seg, n):
    return jax.ops.segment_sum(src, seg, n)
kernel_name = 'mk_cond_seq_d2_seqx_r8_a91543'

def setup_inputs(seed: int=0):
    np.random.seed(seed)
    _w = jnp.asarray

    def _rec_inputs():
        import jax
        import jax.numpy as jnp
        _rk = jax.random.key(seed)
        x = -7.109e-05 + 0.9999 * jax.random.normal(jax.random.fold_in(_rk, 1), (32, 128, 128), jnp.float32)
        _lenS = 128 - jax.random.randint(jax.random.fold_in(_rk, 7), (32,), 0, max(1, 128 // 4) + 1, jnp.int32)
        _lenS2 = 128 - jax.random.randint(jax.random.fold_in(_rk, 8), (32,), 0, max(1, 128 // 4) + 1, jnp.int32)
        itok_B_0_2 = jax.random.randint(jax.random.fold_in(_rk, 11), (32,), 0, 3, jnp.int32)
        itok_B_0_7 = jax.random.randint(jax.random.fold_in(_rk, 12), (32,), 0, 8, jnp.int32)
        return (x, itok_B_0_2, itok_B_0_7)
    x, itok_B_0_2, itok_B_0_7 = _rec_inputs()

    def _L0_cond_setup():
        import jax, jax.numpy as jnp
        import numpy as np
        H = 128
        EPS = 1e-05

        def _gelu(x):
            return jax.nn.gelu(x, approximate=False)
        key = jax.random.key(seed)
        ks = jax.random.split(key, 16)
        s = 1.0 / np.sqrt(H)
        inp = {'x': jax.random.normal(ks[0], (64, 128, H), dtype=jnp.float32), 'condition': jax.random.randint(ks[1], (64,), 0, 3), 'w1_nr': jax.random.normal(ks[2], (H, H), dtype=jnp.float32) * s, 'b1_nr': jnp.zeros((H,), dtype=jnp.float32), 'w2_nr': jax.random.normal(ks[3], (H, H), dtype=jnp.float32) * s, 'b2_nr': jnp.zeros((H,), dtype=jnp.float32), 'w1_tsr': jax.random.normal(ks[4], (H, H), dtype=jnp.float32) * s, 'b1_tsr': jnp.zeros((H,), dtype=jnp.float32), 'w2_tsr': jax.random.normal(ks[5], (H, H), dtype=jnp.float32) * s, 'b2_tsr': jnp.zeros((H,), dtype=jnp.float32), 'w1_sr': jax.random.normal(ks[6], (H, 2 * H), dtype=jnp.float32) * s, 'b1_sr': jnp.zeros((2 * H,), dtype=jnp.float32), 'w2_sr': jax.random.normal(ks[7], (2 * H, H), dtype=jnp.float32) * (1.0 / np.sqrt(2 * H)), 'b2_sr': jnp.zeros((H,), dtype=jnp.float32), 'w3_sr': jax.random.normal(ks[8], (H, H), dtype=jnp.float32) * s, 'b3_sr': jnp.zeros((H,), dtype=jnp.float32), 'gamma': jnp.ones((H,), dtype=jnp.float32), 'beta': jnp.zeros((H,), dtype=jnp.float32)}
        return inp
    _L0_cond_all = _L0_cond_setup()
    _L0_cond_in = {k: v for k, v in _L0_cond_all.items() if k in ('w1_nr', 'b1_nr', 'w2_nr', 'b2_nr', 'w1_tsr', 'b1_tsr', 'w2_tsr', 'b2_tsr', 'w1_sr', 'b1_sr', 'w2_sr', 'b2_sr', 'w3_sr', 'b3_sr', 'gamma', 'beta')}
    del _L0_cond_all

    def _L1_cond_setup():
        import jax, jax.numpy as jnp
        import numpy as np
        E, H, I = (8, 128, 512)
        B, S = (4, 128)
        LN_EPS = 1e-12
        key = jax.random.key(seed)
        ks = jax.random.split(key, 8)
        x = jax.random.normal(ks[0], (B, S, H), dtype=jnp.float32)
        expert_idx = jax.random.randint(ks[1], (B,), 0, E, dtype=jnp.int64)
        Wi = jax.random.normal(ks[2], (E, H, I), dtype=jnp.float32) * 0.02
        bi = jnp.zeros((E, I), dtype=jnp.float32)
        Wo = jax.random.normal(ks[3], (E, I, H), dtype=jnp.float32) * 0.02
        bo = jnp.zeros((E, H), dtype=jnp.float32)
        gamma = jnp.ones((E, H), dtype=jnp.float32)
        beta = jnp.zeros((E, H), dtype=jnp.float32)
        return {'input_tensor': x, 'expert_idx': expert_idx, 'Wi': Wi, 'bi': bi, 'Wo': Wo, 'bo': bo, 'gamma': gamma, 'beta': beta}
    _L1_cond_all = _L1_cond_setup()
    _L1_cond_in = {k: v for k, v in _L1_cond_all.items() if k in ('Wi', 'bi', 'Wo', 'bo', 'gamma', 'beta')}
    del _L1_cond_all
    return {'x': x, 'itok_B_0_2': itok_B_0_2, 'itok_B_0_7': itok_B_0_7, 'L0_cond_w1_nr': _L0_cond_in['w1_nr'], 'L0_cond_b1_nr': _L0_cond_in['b1_nr'], 'L0_cond_w2_nr': _L0_cond_in['w2_nr'], 'L0_cond_b2_nr': _L0_cond_in['b2_nr'], 'L0_cond_w1_tsr': _L0_cond_in['w1_tsr'], 'L0_cond_b1_tsr': _L0_cond_in['b1_tsr'], 'L0_cond_w2_tsr': _L0_cond_in['w2_tsr'], 'L0_cond_b2_tsr': _L0_cond_in['b2_tsr'], 'L0_cond_w1_sr': _L0_cond_in['w1_sr'], 'L0_cond_b1_sr': _L0_cond_in['b1_sr'], 'L0_cond_w2_sr': _L0_cond_in['w2_sr'], 'L0_cond_b2_sr': _L0_cond_in['b2_sr'], 'L0_cond_w3_sr': _L0_cond_in['w3_sr'], 'L0_cond_b3_sr': _L0_cond_in['b3_sr'], 'L0_cond_gamma': _L0_cond_in['gamma'], 'L0_cond_beta': _L0_cond_in['beta'], 'L1_cond_Wi': _L1_cond_in['Wi'], 'L1_cond_bi': _L1_cond_in['bi'], 'L1_cond_Wo': _L1_cond_in['Wo'], 'L1_cond_bo': _L1_cond_in['bo'], 'L1_cond_gamma': _L1_cond_in['gamma'], 'L1_cond_beta': _L1_cond_in['beta']}

def reference(x, itok_B_0_2, itok_B_0_7, L0_cond_w1_nr, L0_cond_b1_nr, L0_cond_w2_nr, L0_cond_b2_nr, L0_cond_w1_tsr, L0_cond_b1_tsr, L0_cond_w2_tsr, L0_cond_b2_tsr, L0_cond_w1_sr, L0_cond_b1_sr, L0_cond_w2_sr, L0_cond_b2_sr, L0_cond_w3_sr, L0_cond_b3_sr, L0_cond_gamma, L0_cond_beta, L1_cond_Wi, L1_cond_bi, L1_cond_Wo, L1_cond_bo, L1_cond_gamma, L1_cond_beta):
    import jax
    import jax.numpy as jnp

    def _L0_cond_ref(x, condition, w1_nr, b1_nr, w2_nr, b2_nr, w1_tsr, b1_tsr, w2_tsr, b2_tsr, w1_sr, b1_sr, w2_sr, b2_sr, w3_sr, b3_sr, gamma, beta):
        import jax, jax.numpy as jnp
        import numpy as np
        H = 128
        EPS = 1e-05

        def _gelu(x):
            return jax.nn.gelu(x, approximate=False)
        out_nr = _gelu(jnp.einsum('bth,hk->btk', x, w1_nr) + b1_nr)
        out_nr = jnp.einsum('bth,hk->btk', out_nr, w2_nr) + b2_nr
        out_tsr = _gelu(jnp.einsum('bth,hk->btk', x, w1_tsr) + b1_tsr)
        out_tsr = jnp.einsum('bth,hk->btk', out_tsr, w2_tsr) + b2_tsr
        h = _gelu(jnp.einsum('bth,hk->btk', x, w1_sr) + b1_sr)
        h = _gelu(jnp.einsum('bth,hk->btk', h, w2_sr) + b2_sr)
        out_sr = jnp.einsum('bth,hk->btk', h, w3_sr) + b3_sr
        c = condition[:, None, None]
        out = jnp.where(c == 0, out_nr, jnp.where(c == 1, out_tsr, jnp.where(c == 2, out_sr, jnp.zeros_like(x))))
        y = x + out
        mu = jnp.mean(y, axis=-1, keepdims=True)
        var = jnp.mean((y - mu) ** 2, axis=-1, keepdims=True)
        return (y - mu) * jax.lax.rsqrt(var + EPS) * gamma + beta

    def _L1_cond_ref(input_tensor, expert_idx, Wi, bi, Wo, bo, gamma, beta):
        import jax, jax.numpy as jnp
        import numpy as np
        E, H, I = (8, 128, 512)
        B, S = (4, 128)
        LN_EPS = 1e-12
        Wi_b = Wi[expert_idx]
        bi_b = bi[expert_idx]
        Wo_b = Wo[expert_idx]
        bo_b = bo[expert_idx]
        g_b = gamma[expert_idx]
        be_b = beta[expert_idx]
        h = jax.nn.gelu(jnp.einsum('bsh,bhi->bsi', input_tensor, Wi_b) + bi_b[:, None, :], approximate=False)
        o = jnp.einsum('bsi,bih->bsh', h, Wo_b) + bo_b[:, None, :]
        r = o + input_tensor
        mu = jnp.mean(r, axis=-1, keepdims=True)
        var = jnp.mean(jnp.square(r - mu), axis=-1, keepdims=True)
        y = (r - mu) * jax.lax.rsqrt(var + LN_EPS)
        return y * g_b[:, None, :] + be_b[:, None, :]
    x = _L0_cond_ref(x, itok_B_0_2, L0_cond_w1_nr, L0_cond_b1_nr, L0_cond_w2_nr, L0_cond_b2_nr, L0_cond_w1_tsr, L0_cond_b1_tsr, L0_cond_w2_tsr, L0_cond_b2_tsr, L0_cond_w1_sr, L0_cond_b1_sr, L0_cond_w2_sr, L0_cond_b2_sr, L0_cond_w3_sr, L0_cond_b3_sr, L0_cond_gamma, L0_cond_beta)
    x = _L1_cond_ref(x, itok_B_0_7, L1_cond_Wi, L1_cond_bi, L1_cond_Wo, L1_cond_bo, L1_cond_gamma, L1_cond_beta)
    return x

_drawn_inputs = setup_inputs


def setup_inputs(seed=0):
    import zlib

    import numpy as np

    out = dict(_drawn_inputs(seed))
    spreads = {'L0_cond_b1_nr': (0.0, 0.1),
     'L0_cond_b2_nr': (0.0, 0.1),
     'L0_cond_b1_tsr': (0.0, 0.1),
     'L0_cond_b2_tsr': (0.0, 0.1),
     'L0_cond_b1_sr': (0.0, 0.362),
     'L0_cond_b2_sr': (0.0, 0.1),
     'L0_cond_b3_sr': (0.0, 0.1),
     'L0_cond_gamma': (1.0, 0.2),
     'L0_cond_beta': (0.0, 0.1),
     'L1_cond_bi': (0.0, 0.36),
     'L1_cond_bo': (0.0, 0.1),
     'L1_cond_gamma': (1.0, 0.2),
     'L1_cond_beta': (0.0, 0.1)}
    factors = {}
    for name, (base, spread) in spreads.items():
        noise = np.random.default_rng([zlib.crc32(name.encode()), seed]).standard_normal(out[name].shape)
        drawn = base * np.exp(spread * noise) if base else spread * noise
        out[name] = jnp.asarray(drawn.astype(out[name].dtype))
    for name, factor in factors.items():
        out[name] = (out[name] * factor).astype(out[name].dtype)
    return out
```

```python
from contextlib import ExitStack

import concourse.bass as bass
from concourse import mybir

P = 128
G = 4
ALU = mybir.AluOpType
ACT = mybir.ActivationFunctionType
F32 = mybir.dt.float32
I32 = mybir.dt.int32

EPS0 = 1e-5
EPS1 = 1e-12


def conditional_then_expert_layers(
    nc, x, cond, expert,
    w1_nr, b1_nr, w2_nr, b2_nr, w1_tsr, b1_tsr, w2_tsr, b2_tsr,
    w1_sr, b1_sr, w2_sr, b2_sr, w3_sr, b3_sr, gamma0, beta0,
    wi, bi, wo, bo, gamma1, beta1, out,
):
    N, S, H = x.shape
    E, _, I = wi.shape
    H2 = w1_sr.shape[1]
    NG = N // G
    KI = I // P
    BR = 4
    assert S == P and H == P and H2 == 2 * P and I == 4 * P and NG % 2 == 0 and NG >= 6

    with ExitStack() as ctx:
        def sb(name, shape, dt=F32):
            return ctx.enter_context(nc.sbuf_tensor(name, shape, dt))

        def psum(name, shape):
            return ctx.enter_context(nc.psum_tensor(name, shape, F32))

        def sem(name):
            return ctx.enter_context(nc.semaphore(name))

        ident = sb("ident", [P, P])
        raw_idx = sb("raw_idx", [P, 2, N], I32)
        idx_tmp = sb("idx_tmp", [P, 2, N], I32)
        branch = sb("branch", [P, N], I32)
        expert_of = sb("expert_of", [P, N], I32)
        is_sr = sb("is_sr", [P, N], I32)
        sr_mask = sb("sr_mask", [P, G], I32)

        x_in = sb("x_in", [P, 2, G, H])
        tok = sb("tok", [P, N, H])
        x1 = sb("x1", [P, G, H])
        x1T = sb("x1T", [P, G, S])
        res1 = sb("res1", [P, N, H])

        w_in = sb("w_in", [P, BR, H2])
        b_in = sb("b_in", [P, BR, H2])
        w_mid = sb("w_mid", [P, 2, H])
        b_mid = sb("b_mid", [P, 1])
        w_last = sb("w_last", [P, BR, H])
        b_last = sb("b_last", [P, BR, H])
        g0_row = sb("g0_row", [P, H])
        be0_row = sb("be0_row", [P, H])
        wi_sb = sb("wi_sb", [P, E, I])
        wo_sb = sb("wo_sb", [P, E, KI, H])
        bi_row = sb("bi_row", [P, E, I])
        bo_row = sb("bo_row", [P, E, H])
        g1_row = sb("g1_row", [P, E, H])
        be1_row = sb("be1_row", [P, E, H])

        xT = sb("xT", [P, G, S])
        pre_in = sb("pre_in", [P, G, H2])
        h_lo = sb("h_lo", [P, 2, G, S])
        h_hi = sb("h_hi", [P, G, S])
        pre_hid = sb("pre_hid", [P, 2, I])
        hidT = sb("hidT", [P, 2, I])
        stats0 = sb("stats0", [P, G, 6])
        mv0 = sb("mv0", [P, G, 2])
        var0 = sb("var0", [P, G])
        rstd0 = sb("rstd0", [P, G])
        eps0 = sb("eps0", [P, G])
        eps1 = sb("eps1", [P, 2])
        minus_half = sb("minus_half", [P, G])
        stats1 = sb("stats1", [P, 2, 6])
        mv1 = sb("mv1", [P, 2, 2])
        var1 = sb("var1", [P, 2])
        rstd1 = sb("rstd1", [P, 2])

        p_xT = psum("p_xT", [P, G, S])
        p_in = [psum(f"p_in{k}", [P, 2 * H2]) for k in range(2)]
        p_hT = [psum(f"p_hT{k}", [P, G * S]) for k in range(2)]
        p_mid = psum("p_mid", [P, G, S])
        p_last = psum("p_last", [P, G, H])
        p_sr = psum("p_sr", [P, G, S])

        idx_loaded = sem("idx_loaded")
        x_loaded = [sem(f"x_loaded{k}") for k in range(2)]
        w0_loaded = sem("w0_loaded")
        wi_loaded = sem("wi_loaded")
        wo_loaded = sem("wo_loaded")
        rows_loaded = sem("rows_loaded")
        zeroed = sem("zeroed")
        ident_made = sem("ident_made")
        idx_step = sem("idx_step")
        idx_ready = sem("idx_ready")
        xT_done = sem("xT_done")
        xT_copied = sem("xT_copied")
        x1T_copied = sem("x1T_copied")
        in_done = sem("in_done")
        in_copied = sem("in_copied")
        hT_done = sem("hT_done")
        h_ready = sem("h_ready")
        mid_done = sem("mid_done")
        sr_ready = sem("sr_ready")
        mask_ready = sem("mask_ready")
        selected = sem("selected")
        last_done = sem("last_done")
        xb_ready = sem("xb_ready")
        last_free = sem("last_free")
        y_ready = sem("y_ready")
        stats0_ready = sem("stats0_ready")
        mv0_ready = sem("mv0_ready")
        var0_ready = sem("var0_ready")
        rstd0_ready = sem("rstd0_ready")
        n_ready = sem("n_ready")
        x1g_ready = sem("x1g_ready")
        x1_ready = sem("x1_ready")
        res1_ready = sem("res1_ready")
        hid_done = sem("hid_done")
        hid_copied = sem("hid_copied")
        hidT_done = sem("hidT_done")
        hidT_ready = sem("hidT_ready")
        o_done = sem("o_done")
        r_ready = sem("r_ready")
        stats1_ready = sem("stats1_ready")
        mv1_ready = sem("mv1_ready")
        var1_ready = sem("var1_ready")
        rstd1_ready = sem("rstd1_ready")
        n1_ready = sem("n1_ready")
        scaled = sem("scaled")
        y1_ready = sem("y1_ready")
        stored = sem("stored")
        sp_passed = sem("sp_passed")
        dve_passed = sem("dve_passed")

        x_dram = x.rearrange("(g j) s h -> g s j h", j=G)
        out_dram = out.rearrange("(g j) s h -> g s j h", j=G)

        def row(ap, n):
            return ap.rearrange("(a n) -> a n", a=1).broadcast_to([P, n])

        def table(ap):
            return ap.rearrange("(a e) n -> a (e n)", a=1).broadcast_to([P, ap.shape[0] * ap.shape[1]])

        def col(ap):
            return ap.rearrange("(h a) -> h a", a=1)

        def wait_alone(eng, s, value, passed):
            eng.wait_ge(s, value)
            eng.sem_inc(passed, 1)

        def group(t, g):
            return t[:, bass.ds(g * G, G), :]

        registers = {}

        def load_values(eng, name, src, first, count, top):
            for k in range(count):
                if f"{name}{k}" not in registers:
                    registers[f"{name}{k}"] = eng.alloc_register(f"{name}{k}")
            regs = [registers[f"{name}{k}"] for k in range(count)]
            eng.load(regs, src[0:1, bass.ds(first, count)])
            return regs, lambda k: eng.snap(regs[k], min_val=0, max_val=top)

        block = ctx.enter_context(nc.Block())

        small_loads = [
            (w_in[:, 0, 0:H], w1_nr), (w_in[:, 1, 0:H], w1_tsr), (w_in[:, 2, :], w1_sr),
            (b_in[:, 0, 0:H], row(b1_nr, H)), (b_in[:, 1, 0:H], row(b1_tsr, H)), (b_in[:, 2, :], row(b1_sr, H2)),
            (w_mid[:], w2_sr.rearrange("(k p) h -> p k h", k=2)), (b_mid[:], col(b2_sr)),
            (w_last[:, 0, :], w2_nr), (w_last[:, 1, :], w2_tsr), (w_last[:, 2, :], w3_sr),
            (b_last[:, 0, :], row(b2_nr, H)), (b_last[:, 1, :], row(b2_tsr, H)), (b_last[:, 2, :], row(b3_sr, H)),
            (g0_row[:], row(gamma0, H)), (be0_row[:], row(beta0, H)),
        ]
        W0 = 16 * len(small_loads)

        @block.sync
        def _(sp):
            sp.dma_start(raw_idx[:, 0, :], row(cond, N)).then_inc(idx_loaded, 16)
            sp.dma_start(raw_idx[:, 1, :], row(expert, N)).then_inc(idx_loaded, 16)
            for par in range(2):
                sp.dma_start(x_in[:, par], x_dram[par]).then_inc(x_loaded[par], 16)

            def load_x(g, par):
                wait_alone(sp, xT_done, g - 1, sp_passed)
                wait_alone(sp, xb_ready, (g - 1) * G, sp_passed)
                sp.dma_start(x_in[:, par], x_dram[bass.ds(g, 1)].rearrange("a s j h -> (a s) j h")).then_inc(x_loaded[par], 16)

            with sp.Fori(2, NG - 1, 2) as g:
                load_x(g, 0)
                load_x(g + 1, 1)
            sp.dma_start(wi_sb[:], wi.rearrange("e h i -> h e i")).then_inc(wi_loaded, 16)
            sp.dma_start(wo_sb[:], wo.rearrange("e (k p) h -> p e k h", k=KI)).then_inc(wo_loaded, 16)
            with sp.Fori(0, NG) as g:
                wait_alone(sp, y1_ready, g * G + G, sp_passed)
                sp.dma_start(out_dram[bass.ds(g, 1)].rearrange("a s j h -> (a s) j h"),
                             group(res1, g)).then_inc(stored, 16)
            sp.wait_ge(stored, 16 * NG)

        @block.gpsimd
        def _(pool):
            nc.gpsimd.memset(ident[:], 0.0).then_inc(zeroed, 1)
            nc.gpsimd.memset(w_in[:], 0.0).then_inc(zeroed, 1)
            nc.gpsimd.memset(b_in[:], 0.0).then_inc(zeroed, 1)
            nc.gpsimd.memset(w_last[:, 3, :], 0.0).then_inc(zeroed, 1)
            nc.gpsimd.memset(b_last[:, 3, :], 0.0).then_inc(zeroed, 1)
            nc.gpsimd.memset(minus_half[:], -0.5).then_inc(zeroed, 1)
            nc.gpsimd.memset(eps0[:], EPS0).then_inc(zeroed, 1)
            nc.gpsimd.memset(eps1[:], EPS1).then_inc(zeroed, 1)
            pool.wait_ge(zeroed, 8)
            nc.gpsimd.affine_select(out=ident[:], in_=ident[:], compare_op=ALU.not_equal, fill=1.0, base=0,
                                    pattern=[[-1, P]], channel_multiplier=1).then_inc(ident_made, 1)
            pool.wait_ge(w0_loaded, W0)
            pool.wait_ge(idx_ready, 1)
            pool.wait_ge(rows_loaded, 64)

            def add_last_bias(g, par):
                _, br = load_values(pool, "pool_br", branch, g * G, G, BR - 1)
                pool.wait_ge(x_loaded[par], 8 * (g - par) + 16)
                for j in range(G):
                    nc.gpsimd.tensor_tensor(out=tok[:, bass.ds(g * G + j, 1), :], in0=x_in[:, par, j:j + 1, :],
                                            in1=b_last[:, bass.ds(br(j), 1), :], op=ALU.add).then_inc(xb_ready, 1)

            def invert_deviation0(g):
                pool.wait_ge(mv0_ready, g * G + G)
                nc.gpsimd.tensor_tensor(out=var0[:], in0=mv0[:, :, 1], in1=eps0[:], op=ALU.add).then_inc(var0_ready, 1)
                pool.wait_ge(var0_ready, g + 1)
                nc.gpsimd.tensor_tensor(out=rstd0[:], in0=var0[:], in1=minus_half[:], op=ALU.pow).then_inc(rstd0_ready, 1)

            def invert_deviation1(u):
                pool.wait_ge(mv1_ready, 2 * u + 2)
                nc.gpsimd.tensor_tensor(out=var1[:], in0=mv1[:, :, 1], in1=eps1[:], op=ALU.add).then_inc(var1_ready, 1)
                pool.wait_ge(var1_ready, u + 1)
                nc.gpsimd.tensor_tensor(out=rstd1[:], in0=var1[:], in1=minus_half[:, 0:2], op=ALU.pow).then_inc(rstd1_ready, 1)

            def expert_input(g, first=False):
                _, ex = load_values(pool, "pool_ex", expert_of, g * G, G, E - 1)
                pool.wait_ge(n_ready, g * G + G)
                if not first:
                    pool.wait_ge(xT_done, NG + g)
                    pool.wait_ge(res1_ready, g * G)
                nc.gpsimd.tensor_tensor(out=x1[:], in0=group(tok, g),
                                        in1=g0_row[:, None, :].broadcast_to([P, G, H]), op=ALU.mult).then_inc(x1g_ready, 1)
                pool.wait_ge(x1g_ready, g + 1)
                nc.gpsimd.tensor_tensor(out=x1[:], in0=x1[:],
                                        in1=be0_row[:, None, :].broadcast_to([P, G, H]), op=ALU.add).then_inc(x1_ready, 1)
                pool.wait_ge(x1_ready, g + 1)
                for j in range(G):
                    nc.gpsimd.tensor_tensor(out=res1[:, bass.ds(g * G + j, 1), :], in0=x1[:, j:j + 1, :],
                                            in1=bo_row[:, bass.ds(ex(j), 1), :], op=ALU.add).then_inc(res1_ready, 1)

            def scale_result(u, e):
                for j in range(2):
                    rj = res1[:, bass.ds(2 * u + j, 1), :]
                    pool.wait_ge(n1_ready, 2 * u + j + 1)
                    nc.gpsimd.tensor_tensor(out=rj, in0=rj, in1=g1_row[:, bass.ds(e[j], 1), :],
                                            op=ALU.mult).then_inc(scaled, 1)
                    pool.wait_ge(scaled, 2 * u + j + 1)
                    nc.gpsimd.tensor_tensor(out=rj, in0=rj, in1=be1_row[:, bass.ds(e[j], 1), :],
                                            op=ALU.add).then_inc(y1_ready, 1)

            add_last_bias(0, 0)
            add_last_bias(1, 1)
            with pool.Fori(2, NG - 1, 2) as g:
                add_last_bias(g, 0)
                invert_deviation0(g - 2)
                add_last_bias(g + 1, 1)
                invert_deviation0(g - 1)
            invert_deviation0(NG - 2)
            expert_input(0, True)
            invert_deviation0(NG - 1)
            expert_input(1)

            def results_of_group(q):
                _, ex = load_values(pool, "pool_fin", expert_of, q * G, G, E - 1)
                e = [ex(j) for j in range(G)]
                for half in range(2):
                    invert_deviation1(2 * q + half)
                    scale_result(2 * q + half, e[2 * half:2 * half + 2])

            with pool.Fori(0, NG - 2) as q:
                expert_input(q + 2)
                results_of_group(q)
            results_of_group(NG - 2)
            results_of_group(NG - 1)

        @block.tensor
        def _(pe):
            def transpose_x(g, par, wait_copied=True):
                pe.wait_ge(x_loaded[par], 8 * (g - par) + 16)
                if wait_copied:
                    pe.wait_ge(xT_copied, g)
                for j in range(G):
                    last = nc.tensor.transpose(p_xT[:, j, :], x_in[:, par, j, :], ident[:])
                last.then_inc(xT_done, 1)

            def first_product(g, wait_slot=True):
                _, br = load_values(pe, "pe_br", branch, g * G, G, BR - 1)
                pe.wait_ge(xT_copied, g + 1)
                for j in range(G):
                    if wait_slot and j % 2 == 0:
                        pe.wait_ge(in_copied, (g - 1) * G + j + 2)
                    nc.tensor.matmul(p_in[j // 2][:, (j % 2) * H2:(j % 2 + 1) * H2], xT[:, j, :],
                                     w_in[:, bass.ds(br(j), 1), :].rearrange("p a h -> p (a h)"),
                                     start=True, stop=True).then_inc(in_done, 1)

            def transpose_h(g, wait_read=True):
                pe.wait_ge(in_copied, (g + 1) * G)
                if wait_read:
                    pe.wait_ge(h_ready, 2 * g)
                for k in range(2):
                    for j in range(G):
                        last = nc.tensor.transpose(p_hT[k][:, j * S:(j + 1) * S], pre_in[:, j, k * P:(k + 1) * P], ident[:])
                    last.then_inc(hT_done, 1)

            def mid_product(g, par, wait_read=True):
                pe.wait_ge(h_ready, 2 * g + 2)
                if wait_read:
                    pe.wait_ge(sr_ready, g)
                nc.tensor.matmul(p_mid[:], w_mid[:, 0, :], h_lo[:, par], start=True, stop=False)
                nc.tensor.matmul(p_mid[:], w_mid[:, 1, :], h_hi[:], start=False, stop=True).then_inc(mid_done, 1)

            def last_product(g, par):
                _, br = load_values(pe, "pe_brl", branch, g * G, G, BR - 1)
                pe.wait_ge(selected, g + 1)
                pe.wait_ge(last_free, g + 1)
                for j in range(G):
                    last = nc.tensor.matmul(p_last[:, j, :], h_lo[:, par, j, :],
                                            w_last[:, bass.ds(br(j), 1), :].rearrange("p a h -> p (a h)"),
                                            start=True, stop=True)
                last.then_inc(last_done, 1)

            pe.wait_ge(ident_made, 1)
            transpose_x(0, 0, False)
            pe.wait_ge(idx_ready, 1)
            pe.wait_ge(w0_loaded, W0)
            first_product(0, False)
            transpose_x(1, 1)
            transpose_h(0, False)

            first_product(1)
            transpose_x(2, 0)
            mid_product(0, 0, False)
            transpose_h(1)

            def step(g, par, more=True):
                first_product(g)
                if more:
                    transpose_x(g + 1, 1 - par)
                last_product(g - 2, par)
                mid_product(g - 1, 1 - par)
                transpose_h(g)

            with pe.Fori(2, NG - 3, 2) as g:
                step(g, 0)
                step(g + 1, 1)
            step(NG - 2, 0)
            step(NG - 1, 1, more=False)
            last_product(NG - 2, 0)
            mid_product(NG - 1, 1)

            def transpose_x1(q):
                pe.wait_ge(x1_ready, q + 1)
                pe.wait_ge(xT_copied, NG)
                if not isinstance(q, int) or q > 0:
                    pe.wait_ge(x1T_copied, 2 * q)
                for j in range(G):
                    last = nc.tensor.transpose(p_xT[:, j, :], x1[:, j, :], ident[:])
                last.then_inc(xT_done, 1)

            def hidden(slot, par, e):
                nc.tensor.matmul(p_in[par][:], x1T[:, slot, :],
                                 wi_sb[:, bass.ds(e, 1), :].rearrange("p a h -> p (a h)"),
                                 start=True, stop=True).then_inc(hid_done, 1)

            def transpose_hidden(i, par, first=False):
                pe.wait_ge(hid_copied, i + 1)
                if first:
                    pe.wait_ge(h_ready, 2 * NG)
                else:
                    pe.wait_ge(hidT_ready, i - 1)
                for k in range(KI):
                    last = nc.tensor.transpose(p_hT[par][:, k * S:(k + 1) * S], pre_hid[:, par, k * P:(k + 1) * P], ident[:])
                last.then_inc(hidT_done, 1)

            def output(i, j, e):
                bank = (p_mid, p_last)[j // 2]
                pe.wait_ge(hidT_ready, i + 1)
                for k in range(KI):
                    mm = nc.tensor.matmul(bank[:, j % 2, :], hidT[:, j % 2, k * S:(k + 1) * S],
                                          wo_sb[:, bass.ds(e, 1), k, :].rearrange("p a h -> p (a h)"),
                                          start=(k == 0), stop=(k == KI - 1))
                mm.then_inc(o_done, 1)

            transpose_x1(0)
            last_product(NG - 1, 1)
            _, e0 = load_values(pe, "pe_e0_", expert_of, 0, 2, E - 1)
            pe.wait_ge(wi_loaded, 16)
            pe.wait_ge(x1T_copied, 1)
            pe.wait_ge(in_copied, N)
            hidden(0, 0, e0(0))
            hidden(1, 1, e0(1))
            transpose_hidden(0, 0, True)
            pe.wait_ge(wo_loaded, 16)

            def group_step(q, more=True, first=False):
                n = G + 2 if more else G
                _, ex = load_values(pe, "pe_ex", expert_of, q * G, n, E - 1)
                e = [ex(k) for k in range(n)]
                for j in range(G):
                    i = q * G + j
                    if j == 0 and more:
                        transpose_x1(q + 1)
                    if j < 2 or more:
                        if j % 2 == 0:
                            pe.wait_ge(x1T_copied, 2 * (q + 1) + (0 if j == 0 else 1))
                        pe.wait_ge(hid_copied, i + 1)
                        hidden((j + 2) % G, j % 2, e[j + 2])
                    if j < 3 or more:
                        transpose_hidden(i + 1, (j + 1) % 2, first and j == 0)
                    if j % 2 == 0:
                        if not first:
                            pe.wait_ge(r_ready, 2 * q + j // 2 - 1)
                        elif j == 0:
                            pe.wait_ge(sr_ready, NG)
                        else:
                            pe.wait_ge(y_ready, NG)
                    output(i, j, e[j])

            group_step(0, first=True)
            with pe.Fori(1, NG - 1) as q:
                group_step(q)
            group_step(NG - 1, more=False)

        @block.scalar
        def _(act):
            act.wait_ge(zeroed, 5)
            for dst, src in small_loads:
                act.dma_start(dst, src).then_inc(w0_loaded, 16)
            act.dma_start(bi_row[:].rearrange("p e i -> p (e i)"), table(bi)).then_inc(rows_loaded, 16)
            act.dma_start(bo_row[:].rearrange("p e i -> p (e i)"), table(bo)).then_inc(rows_loaded, 16)
            act.dma_start(g1_row[:].rearrange("p e i -> p (e i)"), table(gamma1)).then_inc(rows_loaded, 16)
            act.dma_start(be1_row[:].rearrange("p e i -> p (e i)"), table(beta1)).then_inc(rows_loaded, 16)

            def copy_xT(g, first=False):
                act.wait_ge(xT_done, g + 1)
                if not first:
                    act.wait_ge(in_done, g * G)
                nc.scalar.copy(xT[:], p_xT[:]).then_inc(xT_copied, 1)

            def gelu_mid(g, first=False):
                act.wait_ge(mid_done, g + 1)
                if not first:
                    act.wait_ge(selected, g)
                nc.scalar.activation(p_sr[:], p_mid[:], ACT.Gelu, bias=b_mid[:]).then_inc(sr_ready, 1)

            def gelu_in(g, par, use):
                act.wait_ge(hT_done, 2 * g + 1)
                if use:
                    act.wait_ge(last_done, g - 1)
                nc.scalar.activation(h_lo[:, par], p_hT[0][:].rearrange("p (j s) -> p j s", j=G), ACT.Gelu).then_inc(h_ready, 1)
                act.wait_ge(hT_done, 2 * g + 2)
                if not isinstance(g, int) or g > 0:
                    act.wait_ge(mid_done, g)
                nc.scalar.activation(h_hi[:], p_hT[1][:].rearrange("p (j s) -> p j s", j=G), ACT.Gelu).then_inc(h_ready, 1)

            act.wait_ge(w0_loaded, W0)
            copy_xT(0, True)
            copy_xT(1)
            gelu_in(0, 0, False)
            copy_xT(2)
            gelu_mid(0, True)
            gelu_in(1, 1, False)

            def step(g, par, more=True):
                if more:
                    copy_xT(g + 1)
                gelu_mid(g - 1)
                gelu_in(g, par, True)

            with act.Fori(2, NG - 3, 2) as g:
                step(g, 0)
                step(g + 1, 1)
            step(NG - 2, 0)
            step(NG - 1, 1, more=False)
            gelu_mid(NG - 1)

            def copy_x1T(q, half):
                act.wait_ge(xT_done, NG + q + 1)
                if not isinstance(q, int) or q > 0:
                    act.wait_ge(hid_done, (q - 1) * G + 2 * half + 2)
                nc.scalar.copy(x1T[:, 2 * half:2 * half + 2, :], p_xT[:, 2 * half:2 * half + 2, :]).then_inc(x1T_copied, 1)

            def gelu_hidden(i, par, first=False):
                act.wait_ge(hidT_done, i + 1)
                if not first:
                    act.wait_ge(o_done, i - 1)
                nc.scalar.activation(hidT[:, par], p_hT[par][:], ACT.Gelu).then_inc(hidT_ready, 1)

            copy_x1T(0, 0)
            copy_x1T(0, 1)
            gelu_hidden(0, 0, True)

            def group_gelus(q, first=False):
                for j in range(G):
                    gelu_hidden(q * G + j + 1, (j + 1) % 2, first and j == 0)
                    if j < 2:
                        copy_x1T(q + 1, j)

            group_gelus(0, True)
            with act.Fori(1, NG - 1) as q:
                group_gelus(q)
            for j in range(G - 1):
                gelu_hidden(N - G + j + 1, (j + 1) % 2)

        @block.vector
        def _(dve):
            dve.wait_ge(idx_loaded, 32)
            nc.vector.tensor_scalar(idx_tmp[:, 0, :], raw_idx[:, 0, :], 0, 8, ALU.is_lt, ALU.mult).then_inc(idx_step, 1)
            nc.vector.tensor_scalar(idx_tmp[:, 1, :], raw_idx[:, 1, :], 0, E, ALU.is_lt, ALU.mult).then_inc(idx_step, 1)
            nc.vector.tensor_scalar(is_sr[:], raw_idx[:, 0, :], 2, None, ALU.is_equal).then_inc(idx_step, 1)
            nc.vector.tensor_scalar(branch[:], raw_idx[:, 0, :], 0, 3, ALU.max, ALU.min).then_inc(idx_step, 1)
            dve.wait_ge(idx_step, 4)
            nc.vector.tensor_tensor(branch[:], branch[:], idx_tmp[:, 0, :], ALU.add).then_inc(idx_step, 1)
            nc.vector.tensor_tensor(expert_of[:], raw_idx[:, 1, :], idx_tmp[:, 1, :], ALU.add).then_inc(idx_step, 1)
            dve.wait_ge(idx_step, 6)
            nc.vector.tensor_scalar(branch[:], branch[:], 3, None, ALU.min).then_inc(idx_step, 1)
            nc.vector.tensor_scalar(expert_of[:], expert_of[:], 0, E - 1, ALU.max, ALU.min).then_inc(idx_step, 1)
            dve.wait_ge(idx_step, 8)
            nc.vector.nop().then_inc(idx_ready, 1)
            dve.sem_inc(last_free, 1)
            dve.wait_ge(w0_loaded, W0)

            def copy_in(g):
                _, br = load_values(dve, "dve_br", branch, g * G, G, BR - 1)
                if not isinstance(g, int) or g > 0:
                    dve.wait_ge(hT_done, 2 * g)
                for j in range(G):
                    if j % 2 == 0:
                        dve.wait_ge(in_done, g * G + j + 2)
                    nc.vector.tensor_tensor(pre_in[:, j, :], p_in[j // 2][:, (j % 2) * H2:(j % 2 + 1) * H2],
                                            b_in[:, bass.ds(br(j), 1), :].rearrange("p a h -> p (a h)"),
                                            ALU.add).then_inc(in_copied, 1)

            def select(g, par):
                if not isinstance(g, int) or g > 0:
                    dve.wait_ge(selected, g)
                nc.vector.tensor_copy(sr_mask[:], is_sr[:, bass.ds(g * G, G)]).then_inc(mask_ready, 1)
                dve.wait_ge(mask_ready, g + 1)
                wait_alone(dve, sr_ready, g + 1, dve_passed)
                nc.vector.copy_predicated(h_lo[:, par], sr_mask[:, :, None].broadcast_to([P, G, S]), p_sr[:]).then_inc(selected, 1)

            def norm0(g):
                dve.wait_ge(last_done, g + 1)
                dve.wait_ge(xb_ready, g * G + G)
                nc.vector.tensor_tensor(group(tok, g), p_last[:], group(tok, g), ALU.add).then_inc(y_ready, 1)
                wait_alone(dve, y_ready, g + 1, dve_passed)
                dve.sem_inc(last_free, 1)
                for j in range(G):
                    nc.vector.bn_stats(stats0[:, j, :], tok[:, bass.ds(g * G + j, 1), :].rearrange("p a h -> p (a h)")).then_inc(stats0_ready, 1)
                wait_alone(dve, stats0_ready, g * G + G, dve_passed)
                for j in range(G):
                    nc.vector.bn_aggr(mv0[:, j, :], stats0[:, j, :]).then_inc(mv0_ready, 1)
                dve.wait_ge(rstd0_ready, g + 1)
                for j in range(G):
                    tj = tok[:, bass.ds(g * G + j, 1), :]
                    nc.vector.tensor_scalar(tj, tj, mv0[:, j, 0:1], rstd0[:, j:j + 1], ALU.subtract, ALU.mult).then_inc(n_ready, 1)
                dve.wait_ge(n_ready, g * G + G)

            copy_in(0)
            copy_in(1)
            select(0, 0)

            def step(g, par):
                copy_in(g)
                norm0(g - 2)
                select(g - 1, 1 - par)

            with dve.Fori(2, NG - 1, 2) as g:
                step(g, 0)
                step(g + 1, 1)
            norm0(NG - 2)
            select(NG - 1, 1)
            norm0(NG - 1)

            dve.wait_ge(rows_loaded, 64)

            def copy_hidden(i, par, e, first=False):
                dve.wait_ge(hid_done, i + 1)
                if not first:
                    dve.wait_ge(hidT_done, i - 1)
                nc.vector.tensor_tensor(pre_hid[:, par, :], p_in[par][:], bi_row[:, bass.ds(e, 1), :].rearrange("p a i -> p (a i)"),
                                        ALU.add).then_inc(hid_copied, 1)

            def norm1(u, par):
                bank = (p_mid, p_last)[par]
                pair = res1[:, bass.ds(u * 2, 2), :]
                dve.wait_ge(o_done, 2 * u + 2)
                dve.wait_ge(res1_ready, 2 * u + 2)
                nc.vector.tensor_tensor(pair, bank[:, 0:2, :], pair, ALU.add).then_inc(r_ready, 1)
                wait_alone(dve, r_ready, u + 1, dve_passed)
                for j in range(2):
                    nc.vector.bn_stats(stats1[:, j, :], res1[:, bass.ds(2 * u + j, 1), :].rearrange("p a h -> p (a h)")).then_inc(stats1_ready, 1)
                wait_alone(dve, stats1_ready, 2 * u + 2, dve_passed)
                for j in range(2):
                    nc.vector.bn_aggr(mv1[:, j, :], stats1[:, j, :]).then_inc(mv1_ready, 1)
                dve.wait_ge(rstd1_ready, u + 1)
                for j in range(2):
                    rj = res1[:, bass.ds(2 * u + j, 1), :]
                    nc.vector.tensor_scalar(rj, rj, mv1[:, j, 0:1], rstd1[:, j:j + 1], ALU.subtract, ALU.mult).then_inc(n1_ready, 1)
                dve.wait_ge(n1_ready, 2 * u + 2)

            _, ex = load_values(dve, "dve_e0_", expert_of, 0, 2, E - 1)
            copy_hidden(0, 0, ex(0), True)
            copy_hidden(1, 1, ex(1), True)

            def pair_steps(q, more=True):
                n = G if more else 2
                _, ex = load_values(dve, "dve_ex", expert_of, q * G + 2, n, E - 1)
                e = [ex(k) for k in range(n)]
                copy_hidden(q * G + 2, 0, e[0])
                copy_hidden(q * G + 3, 1, e[1])
                norm1(2 * q, 0)
                if more:
                    copy_hidden(q * G + 4, 0, e[2])
                    copy_hidden(q * G + 5, 1, e[3])
                norm1(2 * q + 1, 1)

            with dve.Fori(0, NG - 1) as q:
                pair_steps(q)
            pair_steps(NG - 1, more=False)


_INS = ['x', 'itok_B_0_2', 'itok_B_0_7', 'L0_cond_w1_nr', 'L0_cond_b1_nr', 'L0_cond_w2_nr', 'L0_cond_b2_nr',
        'L0_cond_w1_tsr', 'L0_cond_b1_tsr', 'L0_cond_w2_tsr', 'L0_cond_b2_tsr', 'L0_cond_w1_sr', 'L0_cond_b1_sr',
        'L0_cond_w2_sr', 'L0_cond_b2_sr', 'L0_cond_w3_sr', 'L0_cond_b3_sr', 'L0_cond_gamma', 'L0_cond_beta',
        'L1_cond_Wi', 'L1_cond_bi', 'L1_cond_Wo', 'L1_cond_bo', 'L1_cond_gamma', 'L1_cond_beta']


def kernel(**inputs):
    import numpy as _np
    import concourse.bacc as _bacc
    from concourse import mybir as _mybir
    from concourse.bass_utils import run_bass_kernel_spmd as _run

    nc = _bacc.Bacc("TRN2", target_bir_lowering=False, num_devices=1)
    arrays, args = {}, []
    for name in _INS:
        a = _np.ascontiguousarray(inputs[name])
        arrays[f"in_{name}_dram"] = a
        args.append(nc.dram_tensor(f"in_{name}_dram", a.shape, _mybir.dt.from_np(a.dtype), kind="ExternalInput").ap())
    shape = tuple(inputs["x"].shape)
    args.append(nc.dram_tensor("out_0_dram", shape, _mybir.dt.float32, kind="ExternalOutput").ap())
    conditional_then_expert_layers(nc, *args)
    r = _run(nc, [arrays], core_ids=[0])
    return r.results[0]["out_0_dram"]
```

```python
from contextlib import ExitStack

import concourse.bass as bass
from concourse import mybir

P = 128
G = 4
ALU = mybir.AluOpType
ACT = mybir.ActivationFunctionType
F32 = mybir.dt.float32
I32 = mybir.dt.int32

EPS0 = 1e-5
EPS1 = 1e-12


def conditional_then_expert_layers(nc, x, indices, w0, rows0, b_mid_dram, wi, wo, rows1, out):
    N, S, H = x.shape
    E, _, I = wi.shape
    H2 = 2 * H
    NG = N // G
    KI = I // P
    BR = 4
    assert S == P and H == P and I == 4 * P and NG % 2 == 0 and NG >= 6
    assert w0.shape == (H, 9 * H) and rows0.shape == (9 * H,) and rows1.shape == (E * (I + 3 * H),)

    with ExitStack() as ctx:
        def sb(name, shape, dt=F32):
            return ctx.enter_context(nc.sbuf_tensor(name, shape, dt))

        def psum(name, shape):
            return ctx.enter_context(nc.psum_tensor(name, shape, F32))

        def sem(name):
            return ctx.enter_context(nc.semaphore(name))

        ident = sb("ident", [P, P])
        raw_idx = sb("raw_idx", [P, 2, N], I32)
        idx_tmp = sb("idx_tmp", [P, 2, N], I32)
        branch = sb("branch", [P, N], I32)
        expert_of = sb("expert_of", [P, N], I32)
        is_sr = sb("is_sr", [P, N], I32)
        sr_mask = sb("sr_mask", [P, G], I32)

        x_in = sb("x_in", [P, 2, G, H])
        tok = sb("tok", [P, N, H])
        x1 = sb("x1", [P, G, H])
        x1T = sb("x1T", [P, G, S])
        res1 = sb("res1", [P, N, H])

        w_in = sb("w_in", [P, BR + 1, H])
        w_last = sb("w_last", [P, BR, H])
        w_mid = sb("w_mid", [P, 2, H])
        b_in = sb("b_in", [P, BR + 1, H])
        b_last = sb("b_last", [P, BR, H])
        g_be0 = sb("g_be0", [P, 2, H])
        b_mid = sb("b_mid", [P, 1])
        wi_sb = sb("wi_sb", [P, E, I])
        wo_sb = sb("wo_sb", [P, E, KI, H])
        bi_row = sb("bi_row", [P, E, I])
        bo_row = sb("bo_row", [P, E, H])
        g1_row = sb("g1_row", [P, E, H])
        be1_row = sb("be1_row", [P, E, H])

        xT = sb("xT", [P, G, S])
        pre_in = sb("pre_in", [P, G, H2])
        h_lo = sb("h_lo", [P, 2, G, S])
        h_hi = sb("h_hi", [P, G, S])
        pre_hid = sb("pre_hid", [P, 2, I])
        hidT = sb("hidT", [P, 2, I])
        stats0 = sb("stats0", [P, G, 6])
        mv0 = sb("mv0", [P, 2, G, 2])
        var0 = sb("var0", [P, 2, G])
        rstd0 = sb("rstd0", [P, 2, G])
        stats1 = sb("stats1", [P, 2, 6])
        mv1 = sb("mv1", [P, 2, 2, 2])
        var1 = sb("var1", [P, 2, 2])
        rstd1 = sb("rstd1", [P, 2, 2])
        eps0 = sb("eps0", [P, G])
        eps1 = sb("eps1", [P, 2])
        minus_half = sb("minus_half", [P, G])

        p_xT = psum("p_xT", [P, G, S])
        p_in = [psum(f"p_in{k}", [P, 2 * H2]) for k in range(2)]
        p_hT = [psum(f"p_hT{k}", [P, G * S]) for k in range(2)]
        p_mid = psum("p_mid", [P, G, S])
        p_last = psum("p_last", [P, G, H])
        p_sr = psum("p_sr", [P, G, S])

        idx_loaded = sem("idx_loaded")
        x_loaded = [sem(f"x_loaded{k}") for k in range(2)]
        w_in_loaded = sem("w_in_loaded")
        b_in_loaded = sem("b_in_loaded")
        w0_loaded = sem("w0_loaded")
        wi_loaded = sem("wi_loaded")
        wo_loaded = sem("wo_loaded")
        rows_loaded = sem("rows_loaded")
        zeroed = sem("zeroed")
        ident_made = sem("ident_made")
        idx_step = sem("idx_step")
        idx_ready = sem("idx_ready")
        xT_done = sem("xT_done")
        xT_copied = sem("xT_copied")
        x1T_copied = sem("x1T_copied")
        in_done = sem("in_done")
        in_copied = sem("in_copied")
        hT_done = sem("hT_done")
        h_ready = sem("h_ready")
        mid_done = sem("mid_done")
        sr_ready = sem("sr_ready")
        mask_ready = sem("mask_ready")
        selected = sem("selected")
        last_done = sem("last_done")
        xb_ready = sem("xb_ready")
        last_free = sem("last_free")
        y_ready = sem("y_ready")
        stats0_ready = sem("stats0_ready")
        mv0_ready = sem("mv0_ready")
        var0_ready = sem("var0_ready")
        rstd0_ready = sem("rstd0_ready")
        n_ready = sem("n_ready")
        x1g_ready = sem("x1g_ready")
        x1_ready = sem("x1_ready")
        res1_ready = sem("res1_ready")
        hid_done = sem("hid_done")
        hid_copied = sem("hid_copied")
        hidT_done = sem("hidT_done")
        hidT_ready = sem("hidT_ready")
        o_done = sem("o_done")
        r_ready = sem("r_ready")
        stats1_ready = sem("stats1_ready")
        mv1_ready = sem("mv1_ready")
        var1_ready = sem("var1_ready")
        rstd1_ready = sem("rstd1_ready")
        n1_ready = sem("n1_ready")
        centred = sem("centred")
        y1_ready = sem("y1_ready")
        stored = sem("stored")
        sp_passed = sem("sp_passed")
        dve_passed = sem("dve_passed")

        x_dram = x.rearrange("(g j) s h -> g s j h", j=G)
        out_dram = out.rearrange("(g j) s h -> g s j h", j=G)

        def wait_alone(eng, s, value, passed):
            eng.wait_ge(s, value)
            eng.sem_inc(passed, 1)

        def group(t, g):
            return t[:, bass.ds(g * G, G), :]

        registers = {}

        def load_values(eng, name, src, first, count, top):
            for k in range(count):
                if f"{name}{k}" not in registers:
                    registers[f"{name}{k}"] = eng.alloc_register(f"{name}{k}")
            regs = [registers[f"{name}{k}"] for k in range(count)]
            eng.load(regs, src[0:1, bass.ds(first, count)])
            return regs, lambda k: eng.snap(regs[k], min_val=0, max_val=top)

        block = ctx.enter_context(nc.Block())

        def row(ap, first, n):
            return ap[first:first + n].rearrange("(a n) -> a n", a=1).broadcast_to([P, n])

        def flat(t):
            return t.rearrange("p a h -> p (a h)")

        W0 = 5 * 16
        ZEROED = 8

        @block.sync
        def _(sp):
            sp.dma_start(flat(raw_idx[:]), indices.rearrange("(a b) n -> a (b n)", a=1).broadcast_to([P, 2 * N])).then_inc(idx_loaded, 16)
            for par in range(2):
                sp.dma_start(x_in[:, par], x_dram[par]).then_inc(x_loaded[par], 16)
            sp.dma_start(flat(w_last[:, 0:3, :]), w0[:, 4 * H:7 * H]).then_inc(w0_loaded, 16)
            sp.dma_start(flat(g_be0[:]), row(rows0, 7 * H, 2 * H)).then_inc(w0_loaded, 16)

            def load_x(g, par):
                wait_alone(sp, xT_done, g - 1, sp_passed)
                wait_alone(sp, xb_ready, (g - 1) * G, sp_passed)
                sp.dma_start(x_in[:, par], x_dram[bass.ds(g, 1)].rearrange("a s j h -> (a s) j h")).then_inc(x_loaded[par], 16)

            with sp.Fori(2, NG - 1, 2) as g:
                load_x(g, 0)
                load_x(g + 1, 1)
            sp.dma_start(wi_sb[:], wi.rearrange("e h i -> h e i")).then_inc(wi_loaded, 16)
            sp.dma_start(wo_sb[:], wo.rearrange("e (k p) h -> p e k h", k=KI)).then_inc(wo_loaded, 16)
            with sp.Fori(0, NG) as g:
                wait_alone(sp, y1_ready, g * G + G, sp_passed)
                sp.dma_start(out_dram[bass.ds(g, 1)].rearrange("a s j h -> (a s) j h"),
                             group(res1, g)).then_inc(stored, 16)
            sp.wait_ge(stored, 16 * NG)

        @block.gpsimd
        def _(pool):
            nc.gpsimd.memset(ident[:], 0.0).then_inc(zeroed, 1)
            pool.wait_ge(zeroed, 1)
            nc.gpsimd.affine_select(out=ident[:], in_=ident[:], compare_op=ALU.not_equal, fill=1.0, base=0,
                                    pattern=[[-1, P]], channel_multiplier=1).then_inc(ident_made, 1)
            nc.gpsimd.memset(w_in[:, BR, :], 0.0).then_inc(zeroed, 1)
            nc.gpsimd.memset(b_in[:, BR, :], 0.0).then_inc(zeroed, 1)
            nc.gpsimd.memset(w_last[:, 3, :], 0.0).then_inc(zeroed, 1)
            nc.gpsimd.memset(b_last[:, 3, :], 0.0).then_inc(zeroed, 1)
            nc.gpsimd.memset(minus_half[:], -0.5).then_inc(zeroed, 1)
            nc.gpsimd.memset(eps0[:], EPS0).then_inc(zeroed, 1)
            nc.gpsimd.memset(eps1[:], EPS1).then_inc(zeroed, 1)
            pool.wait_ge(zeroed, ZEROED)
            pool.wait_ge(w0_loaded, W0)
            pool.wait_ge(idx_ready, 1)

            def add_last_bias(g, par):
                _, br = load_values(pool, "pool_br", branch, g * G, G, BR - 1)
                pool.wait_ge(x_loaded[par], 8 * (g - par) + 16)
                for j in range(G):
                    nc.gpsimd.tensor_tensor(out=tok[:, bass.ds(g * G + j, 1), :], in0=x_in[:, par, j:j + 1, :],
                                            in1=b_last[:, bass.ds(br(j), 1), :], op=ALU.add).then_inc(xb_ready, 1)

            def invert_deviation0(g, par, reuse=True):
                if reuse:
                    pool.wait_ge(n_ready, (g - 1) * G)
                pool.wait_ge(mv0_ready, g * G + G)
                nc.gpsimd.tensor_tensor(out=var0[:, par, :], in0=mv0[:, par, :, 1], in1=eps0[:], op=ALU.add).then_inc(var0_ready, 1)
                pool.wait_ge(var0_ready, g + 1)
                nc.gpsimd.tensor_tensor(out=rstd0[:, par, :], in0=var0[:, par, :], in1=minus_half[:], op=ALU.pow).then_inc(rstd0_ready, 1)

            def invert_deviation1(u, par, reuse=True):
                if reuse:
                    pool.wait_ge(y1_ready, 2 * u - 2)
                pool.wait_ge(mv1_ready, 2 * u + 2)
                nc.gpsimd.tensor_tensor(out=var1[:, par, :], in0=mv1[:, par, :, 1], in1=eps1[:], op=ALU.add).then_inc(var1_ready, 1)
                pool.wait_ge(var1_ready, u + 1)
                nc.gpsimd.tensor_tensor(out=rstd1[:, par, :], in0=var1[:, par, :], in1=minus_half[:, 0:2], op=ALU.pow).then_inc(rstd1_ready, 1)

            def expert_input(g, first=False):
                _, ex = load_values(pool, "pool_ex", expert_of, g * G, G, E - 1)
                pool.wait_ge(n_ready, g * G + G)
                if not first:
                    pool.wait_ge(xT_done, NG + g)
                    pool.wait_ge(res1_ready, g * G)
                nc.gpsimd.tensor_tensor(out=x1[:], in0=group(tok, g),
                                        in1=g_be0[:, 0:1, :].broadcast_to([P, G, H]), op=ALU.mult).then_inc(x1g_ready, 1)
                pool.wait_ge(x1g_ready, g + 1)
                nc.gpsimd.tensor_tensor(out=x1[:], in0=x1[:],
                                        in1=g_be0[:, 1:2, :].broadcast_to([P, G, H]), op=ALU.add).then_inc(x1_ready, 1)
                pool.wait_ge(x1_ready, g + 1)
                for j in range(G):
                    nc.gpsimd.tensor_tensor(out=res1[:, bass.ds(g * G + j, 1), :], in0=x1[:, j:j + 1, :],
                                            in1=bo_row[:, bass.ds(ex(j), 1), :], op=ALU.add).then_inc(res1_ready, 1)

            add_last_bias(0, 0)
            add_last_bias(1, 1)
            add_last_bias(2, 0)
            invert_deviation0(0, 0, False)
            add_last_bias(3, 1)
            invert_deviation0(1, 1, False)
            with pool.Fori(4, NG - 1, 2) as g:
                add_last_bias(g, 0)
                invert_deviation0(g - 2, 0)
                add_last_bias(g + 1, 1)
                invert_deviation0(g - 1, 1)
            pool.wait_ge(rows_loaded, 64)
            invert_deviation0(NG - 2, 0)
            expert_input(0, True)
            invert_deviation0(NG - 1, 1)
            expert_input(1)
            expert_input(2)
            invert_deviation1(0, 0, False)
            invert_deviation1(1, 1, False)
            with pool.Fori(1, NG - 2) as q:
                expert_input(q + 2)
                invert_deviation1(2 * q, 0)
                invert_deviation1(2 * q + 1, 1)
            for u in range(NG * 2 - 4, NG * 2):
                invert_deviation1(u, u % 2)

        @block.tensor
        def _(pe):
            def transpose_x(g, par, wait_copied=True):
                pe.wait_ge(x_loaded[par], 8 * (g - par) + 16)
                if wait_copied:
                    pe.wait_ge(xT_copied, g)
                for j in range(G):
                    last = nc.tensor.transpose(p_xT[:, j, :], x_in[:, par, j, :], ident[:])
                last.then_inc(xT_done, 1)

            def first_product(g, wait_slot=True):
                _, br = load_values(pe, "pe_br", branch, g * G, G, BR - 1)
                pe.wait_ge(xT_copied, g + 1)
                for j in range(G):
                    if wait_slot and j % 2 == 0:
                        pe.wait_ge(in_copied, (g - 1) * G + j + 2)
                    nc.tensor.matmul(p_in[j // 2][:, (j % 2) * H2:(j % 2 + 1) * H2], xT[:, j, :],
                                     flat(w_in[:, bass.ds(br(j), 2), :]),
                                     start=True, stop=True).then_inc(in_done, 1)

            def transpose_h(g, wait_read=True):
                pe.wait_ge(in_copied, (g + 1) * G)
                if wait_read:
                    pe.wait_ge(h_ready, 2 * g)
                for k in range(2):
                    for j in range(G):
                        last = nc.tensor.transpose(p_hT[k][:, j * S:(j + 1) * S], pre_in[:, j, k * P:(k + 1) * P], ident[:])
                    last.then_inc(hT_done, 1)

            def mid_product(g, par, wait_read=True):
                pe.wait_ge(h_ready, 2 * g + 2)
                if wait_read:
                    pe.wait_ge(sr_ready, g)
                nc.tensor.matmul(p_mid[:], w_mid[:, 0, :], h_lo[:, par], start=True, stop=False)
                nc.tensor.matmul(p_mid[:], w_mid[:, 1, :], h_hi[:], start=False, stop=True).then_inc(mid_done, 1)

            def last_product(g, par):
                _, br = load_values(pe, "pe_brl", branch, g * G, G, BR - 1)
                pe.wait_ge(selected, g + 1)
                pe.wait_ge(last_free, g + 1)
                for j in range(G):
                    last = nc.tensor.matmul(p_last[:, j, :], h_lo[:, par, j, :],
                                            w_last[:, bass.ds(br(j), 1), :].rearrange("p a h -> p (a h)"),
                                            start=True, stop=True)
                last.then_inc(last_done, 1)

            pe.wait_ge(ident_made, 1)
            transpose_x(0, 0, False)
            pe.wait_ge(idx_ready, 1)
            pe.wait_ge(w_in_loaded, 16)
            pe.wait_ge(zeroed, ZEROED)
            first_product(0, False)
            transpose_x(1, 1)
            transpose_h(0, False)

            first_product(1)
            transpose_x(2, 0)
            pe.wait_ge(w0_loaded, W0)
            mid_product(0, 0, False)
            transpose_h(1)

            def step(g, par, more=True):
                first_product(g)
                if more:
                    transpose_x(g + 1, 1 - par)
                last_product(g - 2, par)
                mid_product(g - 1, 1 - par)
                transpose_h(g)

            with pe.Fori(2, NG - 3, 2) as g:
                step(g, 0)
                step(g + 1, 1)
            step(NG - 2, 0)
            step(NG - 1, 1, more=False)
            last_product(NG - 2, 0)
            mid_product(NG - 1, 1)

            def transpose_x1(q):
                pe.wait_ge(x1_ready, q + 1)
                pe.wait_ge(xT_copied, NG)
                if not isinstance(q, int) or q > 0:
                    pe.wait_ge(x1T_copied, 2 * q)
                for j in range(G):
                    last = nc.tensor.transpose(p_xT[:, j, :], x1[:, j, :], ident[:])
                last.then_inc(xT_done, 1)

            def hidden(slot, par, e):
                nc.tensor.matmul(p_in[par][:], x1T[:, slot, :],
                                 flat(wi_sb[:, bass.ds(e, 1), :]),
                                 start=True, stop=True).then_inc(hid_done, 1)

            def transpose_hidden(i, par, first=False):
                pe.wait_ge(hid_copied, i + 1)
                if first:
                    pe.wait_ge(h_ready, 2 * NG)
                else:
                    pe.wait_ge(hidT_ready, i - 1)
                for k in range(KI):
                    last = nc.tensor.transpose(p_hT[par][:, k * S:(k + 1) * S], pre_hid[:, par, k * P:(k + 1) * P], ident[:])
                last.then_inc(hidT_done, 1)

            def output(i, j, e):
                bank = (p_mid, p_last)[j // 2]
                pe.wait_ge(hidT_ready, i + 1)
                for k in range(KI):
                    mm = nc.tensor.matmul(bank[:, j % 2, :], hidT[:, j % 2, k * S:(k + 1) * S],
                                          wo_sb[:, bass.ds(e, 1), k, :].rearrange("p a h -> p (a h)"),
                                          start=(k == 0), stop=(k == KI - 1))
                mm.then_inc(o_done, 1)

            transpose_x1(0)
            last_product(NG - 1, 1)
            _, e0 = load_values(pe, "pe_e0_", expert_of, 0, 2, E - 1)
            pe.wait_ge(wi_loaded, 16)
            pe.wait_ge(x1T_copied, 1)
            pe.wait_ge(in_copied, N)
            hidden(0, 0, e0(0))
            hidden(1, 1, e0(1))
            transpose_hidden(0, 0, True)
            pe.wait_ge(wo_loaded, 16)

            def group_step(q, more=True, first=False):
                n = G + 2 if more else G
                _, ex = load_values(pe, "pe_ex", expert_of, q * G, n, E - 1)
                e = [ex(k) for k in range(n)]
                for j in range(G):
                    i = q * G + j
                    if j == 0 and more:
                        transpose_x1(q + 1)
                    if j < 2 or more:
                        if j % 2 == 0:
                            pe.wait_ge(x1T_copied, 2 * (q + 1) + (0 if j == 0 else 1))
                        pe.wait_ge(hid_copied, i + 1)
                        hidden((j + 2) % G, j % 2, e[j + 2])
                    if j < 3 or more:
                        transpose_hidden(i + 1, (j + 1) % 2, first and j == 0)
                    if j % 2 == 0:
                        if not first:
                            pe.wait_ge(r_ready, 2 * q + j // 2 - 1)
                        elif j == 0:
                            pe.wait_ge(sr_ready, NG)
                        else:
                            pe.wait_ge(y_ready, NG)
                    output(i, j, e[j])

            group_step(0, first=True)
            with pe.Fori(1, NG - 1) as q:
                group_step(q)
            group_step(NG - 1, more=False)

        @block.scalar
        def _(act):
            act.dma_start(flat(w_in[:, 0:4, :]), w0[:, 0:4 * H]).then_inc(w_in_loaded, 16)
            act.dma_start(flat(b_in[:, 0:4, :]), row(rows0, 0, 4 * H)).then_inc(b_in_loaded, 16)
            act.dma_start(flat(w_mid[:]), w0[:, 7 * H:9 * H]).then_inc(w0_loaded, 16)
            act.dma_start(b_mid[:], b_mid_dram.rearrange("(h a) -> h a", a=1)).then_inc(w0_loaded, 16)
            act.dma_start(flat(b_last[:, 0:3, :]), row(rows0, 4 * H, 3 * H)).then_inc(w0_loaded, 16)
            act.dma_start(flat(bi_row[:]), row(rows1, 0, E * I)).then_inc(rows_loaded, 16)
            for k, t in enumerate((bo_row, g1_row, be1_row)):
                act.dma_start(flat(t[:]), row(rows1, E * (I + k * H), E * H)).then_inc(rows_loaded, 16)

            def copy_xT(g, first=False):
                act.wait_ge(xT_done, g + 1)
                if not first:
                    act.wait_ge(in_done, g * G)
                nc.scalar.copy(xT[:], p_xT[:]).then_inc(xT_copied, 1)

            def gelu_mid(g, first=False):
                act.wait_ge(mid_done, g + 1)
                if not first:
                    act.wait_ge(selected, g)
                nc.scalar.activation(p_sr[:], p_mid[:], ACT.Gelu, bias=b_mid[:]).then_inc(sr_ready, 1)

            def gelu_in(g, par, use):
                act.wait_ge(hT_done, 2 * g + 1)
                if use:
                    act.wait_ge(last_done, g - 1)
                nc.scalar.activation(h_lo[:, par], p_hT[0][:].rearrange("p (j s) -> p j s", j=G), ACT.Gelu).then_inc(h_ready, 1)
                act.wait_ge(hT_done, 2 * g + 2)
                if not isinstance(g, int) or g > 0:
                    act.wait_ge(mid_done, g)
                nc.scalar.activation(h_hi[:], p_hT[1][:].rearrange("p (j s) -> p j s", j=G), ACT.Gelu).then_inc(h_ready, 1)

            copy_xT(0, True)
            copy_xT(1)
            gelu_in(0, 0, False)
            copy_xT(2)
            act.wait_ge(w0_loaded, W0)
            gelu_mid(0, True)
            gelu_in(1, 1, False)

            def step(g, par, more=True):
                if more:
                    copy_xT(g + 1)
                gelu_mid(g - 1)
                gelu_in(g, par, True)

            with act.Fori(2, NG - 3, 2) as g:
                step(g, 0)
                step(g + 1, 1)
            step(NG - 2, 0)
            step(NG - 1, 1, more=False)
            gelu_mid(NG - 1)

            def copy_x1T(q, half):
                act.wait_ge(xT_done, NG + q + 1)
                if not isinstance(q, int) or q > 0:
                    act.wait_ge(hid_done, (q - 1) * G + 2 * half + 2)
                nc.scalar.copy(x1T[:, 2 * half:2 * half + 2, :], p_xT[:, 2 * half:2 * half + 2, :]).then_inc(x1T_copied, 1)

            def gelu_hidden(i, par, first=False):
                act.wait_ge(hidT_done, i + 1)
                if not first:
                    act.wait_ge(o_done, i - 1)
                nc.scalar.activation(hidT[:, par], p_hT[par][:], ACT.Gelu).then_inc(hidT_ready, 1)

            copy_x1T(0, 0)
            copy_x1T(0, 1)
            gelu_hidden(0, 0, True)

            def group_gelus(q, first=False):
                for j in range(G):
                    gelu_hidden(q * G + j + 1, (j + 1) % 2, first and j == 0)
                    if j < 2:
                        copy_x1T(q + 1, j)

            group_gelus(0, True)
            with act.Fori(1, NG - 1) as q:
                group_gelus(q)
            for j in range(G - 1):
                gelu_hidden(N - G + j + 1, (j + 1) % 2)

        @block.vector
        def _(dve):
            dve.wait_ge(idx_loaded, 16)
            nc.vector.tensor_scalar(idx_tmp[:, 0, :], raw_idx[:, 0, :], 0, 8, ALU.is_lt, ALU.mult).then_inc(idx_step, 1)
            nc.vector.tensor_scalar(idx_tmp[:, 1, :], raw_idx[:, 1, :], 0, E, ALU.is_lt, ALU.mult).then_inc(idx_step, 1)
            nc.vector.tensor_scalar(is_sr[:], raw_idx[:, 0, :], 2, None, ALU.is_equal).then_inc(idx_step, 1)
            nc.vector.tensor_scalar(branch[:], raw_idx[:, 0, :], 0, 3, ALU.max, ALU.min).then_inc(idx_step, 1)
            dve.wait_ge(idx_step, 4)
            nc.vector.tensor_tensor(branch[:], branch[:], idx_tmp[:, 0, :], ALU.add).then_inc(idx_step, 1)
            nc.vector.tensor_tensor(expert_of[:], raw_idx[:, 1, :], idx_tmp[:, 1, :], ALU.add).then_inc(idx_step, 1)
            dve.wait_ge(idx_step, 6)
            nc.vector.tensor_scalar(branch[:], branch[:], 3, None, ALU.min).then_inc(idx_step, 1)
            nc.vector.tensor_scalar(expert_of[:], expert_of[:], 0, E - 1, ALU.max, ALU.min).then_inc(idx_step, 1)
            dve.wait_ge(idx_step, 8)
            nc.vector.nop().then_inc(idx_ready, 1)
            dve.sem_inc(last_free, 1)
            dve.wait_ge(b_in_loaded, 16)
            dve.wait_ge(zeroed, ZEROED)

            def copy_in(g):
                _, br = load_values(dve, "dve_br", branch, g * G, G, BR - 1)
                if not isinstance(g, int) or g > 0:
                    dve.wait_ge(hT_done, 2 * g)
                for j in range(G):
                    if j % 2 == 0:
                        dve.wait_ge(in_done, g * G + j + 2)
                    nc.vector.tensor_tensor(pre_in[:, j, :], p_in[j // 2][:, (j % 2) * H2:(j % 2 + 1) * H2],
                                            flat(b_in[:, bass.ds(br(j), 2), :]),
                                            ALU.add).then_inc(in_copied, 1)

            def select(g, par):
                if not isinstance(g, int) or g > 0:
                    dve.wait_ge(selected, g)
                nc.vector.tensor_copy(sr_mask[:], is_sr[:, bass.ds(g * G, G)]).then_inc(mask_ready, 1)
                dve.wait_ge(mask_ready, g + 1)
                wait_alone(dve, sr_ready, g + 1, dve_passed)
                nc.vector.copy_predicated(h_lo[:, par], sr_mask[:, :, None].broadcast_to([P, G, S]), p_sr[:]).then_inc(selected, 1)

            def moments0(g, par):
                dve.wait_ge(last_done, g + 1)
                dve.wait_ge(xb_ready, g * G + G)
                nc.vector.tensor_tensor(group(tok, g), p_last[:], group(tok, g), ALU.add).then_inc(y_ready, 1)
                wait_alone(dve, y_ready, g + 1, dve_passed)
                dve.sem_inc(last_free, 1)
                for j in range(G):
                    nc.vector.bn_stats(stats0[:, j, :], flat(tok[:, bass.ds(g * G + j, 1), :])).then_inc(stats0_ready, 1)
                wait_alone(dve, stats0_ready, g * G + G, dve_passed)
                for j in range(G):
                    nc.vector.bn_aggr(mv0[:, par, j, :], stats0[:, j, :]).then_inc(mv0_ready, 1)

            def norm0(g, par):
                dve.wait_ge(rstd0_ready, g + 1)
                for j in range(G):
                    tj = tok[:, bass.ds(g * G + j, 1), :]
                    nc.vector.tensor_scalar(tj, tj, mv0[:, par, j, 0:1], rstd0[:, par, j:j + 1],
                                            ALU.subtract, ALU.mult).then_inc(n_ready, 1)

            copy_in(0)
            copy_in(1)
            select(0, 0)

            def step(g, par, norm=True):
                copy_in(g)
                moments0(g - 2, par)
                select(g - 1, 1 - par)
                if norm:
                    norm0(g - 3, 1 - par)

            step(2, 0, norm=False)
            step(3, 1)
            with dve.Fori(4, NG - 1, 2) as g:
                step(g, 0)
                step(g + 1, 1)
            moments0(NG - 2, 0)
            select(NG - 1, 1)
            norm0(NG - 3, 1)
            moments0(NG - 1, 1)
            norm0(NG - 2, 0)

            dve.wait_ge(rows_loaded, 64)

            def copy_hidden(i, par, e, first=False):
                dve.wait_ge(hid_done, i + 1)
                if not first:
                    dve.wait_ge(hidT_done, i - 1)
                nc.vector.tensor_tensor(pre_hid[:, par, :], p_in[par][:], bi_row[:, bass.ds(e, 1), :].rearrange("p a i -> p (a i)"),
                                        ALU.add).then_inc(hid_copied, 1)

            def moments1(u, par):
                bank = (p_mid, p_last)[par]
                pair = res1[:, bass.ds(u * 2, 2), :]
                dve.wait_ge(o_done, 2 * u + 2)
                dve.wait_ge(res1_ready, 2 * u + 2)
                nc.vector.tensor_tensor(pair, bank[:, 0:2, :], pair, ALU.add).then_inc(r_ready, 1)
                wait_alone(dve, r_ready, u + 1, dve_passed)
                for j in range(2):
                    nc.vector.bn_stats(stats1[:, j, :], flat(res1[:, bass.ds(2 * u + j, 1), :])).then_inc(stats1_ready, 1)
                wait_alone(dve, stats1_ready, 2 * u + 2, dve_passed)
                for j in range(2):
                    nc.vector.bn_aggr(mv1[:, par, j, :], stats1[:, j, :]).then_inc(mv1_ready, 1)

            def result(u, par, e):
                for j in range(2):
                    rj = res1[:, bass.ds(2 * u + j, 1), :]
                    nc.vector.scalar_tensor_tensor(out=rj, in0=rj, scalar=mv1[:, par, j, 0:1],
                                                   in1=g1_row[:, bass.ds(e[j], 1), :],
                                                   op0=ALU.subtract, op1=ALU.mult).then_inc(centred, 1)
                dve.wait_ge(rstd1_ready, u + 1)
                dve.wait_ge(centred, 2 * u + 2)
                for j in range(2):
                    rj = res1[:, bass.ds(2 * u + j, 1), :]
                    nc.vector.scalar_tensor_tensor(out=rj, in0=rj, scalar=rstd1[:, par, j:j + 1],
                                                   in1=be1_row[:, bass.ds(e[j], 1), :],
                                                   op0=ALU.mult, op1=ALU.add).then_inc(y1_ready, 1)

            _, ex = load_values(dve, "dve_e0_", expert_of, 0, 2, E - 1)
            copy_hidden(0, 0, ex(0), True)
            copy_hidden(1, 1, ex(1), True)
            norm0(NG - 1, 1)

            def group_step(q, first=False, last=False):
                low = 0 if first else G
                n = low + (G if last else G + 2)
                _, ex = load_values(dve, "dve_ex", expert_of, q * G - low, n, E - 1)
                e = {k - low: ex(k) for k in range(n) if k < low or k >= low + 2}
                copy_hidden(q * G + 2, 0, e[2])
                if not first:
                    moments1(2 * q - 1, 1)
                copy_hidden(q * G + 3, 1, e[3])
                if not first:
                    result(2 * q - 2, 0, (e[-4], e[-3]))
                if not last:
                    copy_hidden(q * G + 4, 0, e[4])
                moments1(2 * q, 0)
                if not last:
                    copy_hidden(q * G + 5, 1, e[5])
                if not first:
                    result(2 * q - 1, 1, (e[-2], e[-1]))

            group_step(0, first=True)
            with dve.Fori(1, NG - 1) as q:
                group_step(q)
            group_step(NG - 1, last=True)
            _, ex = load_values(dve, "dve_ex", expert_of, N - G, G, E - 1)
            e = [ex(k) for k in range(G)]
            moments1(2 * NG - 1, 1)
            result(2 * NG - 2, 0, e[0:2])
            result(2 * NG - 1, 1, e[2:4])


def kernel(**inputs):
    import numpy as _np
    import concourse.bacc as _bacc
    from concourse import mybir as _mybir
    from concourse.bass_utils import run_bass_kernel_spmd as _run

    a0 = {k[len("L0_cond_"):]: _np.asarray(v) for k, v in inputs.items() if k.startswith("L0_cond_")}
    a1 = {k[len("L1_cond_"):]: _np.asarray(v) for k, v in inputs.items() if k.startswith("L1_cond_")}
    h = a0["w1_nr"].shape[0]
    laid_out = {
        "x": _np.asarray(inputs["x"]),
        "indices": _np.stack([_np.asarray(inputs["itok_B_0_2"]), _np.asarray(inputs["itok_B_0_7"])]),
        "w0": _np.concatenate([a0["w1_nr"], a0["w1_tsr"], a0["w1_sr"], a0["w2_nr"], a0["w2_tsr"], a0["w3_sr"],
                               a0["w2_sr"][:h], a0["w2_sr"][h:]], axis=1),
        "rows0": _np.concatenate([a0["b1_nr"], a0["b1_tsr"], a0["b1_sr"], a0["b2_nr"], a0["b2_tsr"], a0["b3_sr"],
                                  a0["gamma"], a0["beta"]]),
        "b_mid": a0["b2_sr"],
        "wi": a1["Wi"],
        "wo": a1["Wo"],
        "rows1": _np.concatenate([a1["bi"].ravel(), a1["bo"].ravel(), a1["gamma"].ravel(), a1["beta"].ravel()]),
    }
    nc = _bacc.Bacc("TRN2", target_bir_lowering=False, num_devices=1)
    arrays, args = {}, []
    for name, a in laid_out.items():
        a = _np.ascontiguousarray(a)
        arrays[f"in_{name}_dram"] = a
        args.append(nc.dram_tensor(f"in_{name}_dram", a.shape, _mybir.dt.from_np(a.dtype), kind="ExternalInput").ap())
    args.append(nc.dram_tensor("out_0_dram", laid_out["x"].shape, _mybir.dt.float32, kind="ExternalOutput").ap())
    conditional_then_expert_layers(nc, *args)
    r = _run(nc, [arrays], core_ids=[0])
    return r.results[0]["out_0_dram"]
```

```python
from contextlib import ExitStack

import concourse.bass as bass
from concourse import mybir

P = 128
G = 4
ALU = mybir.AluOpType
ACT = mybir.ActivationFunctionType
F32 = mybir.dt.float32
I32 = mybir.dt.int32

EPS0 = 1e-5
EPS1 = 1e-12


def conditional_then_expert_layers(nc, x, indices, w0, rows0, cols0_dram, wi, wo, b_hid_dram, rows1, out):
    N, S, H = x.shape
    _, E, I = wi.shape
    NG = N // G
    KI = I // P
    BR = 4
    SR = 2
    AHEAD = 3
    assert S == P and H == P and I == 4 * P and NG % 2 == 0 and NG >= 6
    assert w0.shape == (H, 9 * H) and rows0.shape == (5 * H,) and rows1.shape == (3 * E * H,)

    with ExitStack() as ctx:
        def sb(name, shape, dt=F32):
            return ctx.enter_context(nc.sbuf_tensor(name, shape, dt))

        def psum(name, shape):
            return ctx.enter_context(nc.psum_tensor(name, shape, F32))

        def sem(name):
            return ctx.enter_context(nc.semaphore(name))

        ident = sb("ident", [P, P])
        raw_idx = sb("raw_idx", [P, 2, N], I32)
        idx_tmp = sb("idx_tmp", [1, 2, N], I32)
        is_sr = sb("is_sr", [P, N + G], I32)
        sr_mask = sb("sr_mask", [P, G], I32)
        branch = sb("branch", [1, N + 2 * G], I32)
        expert_of = sb("expert_of", [1, N], I32)

        x_in = sb("x_in", [P, 2, G, H])
        tok = sb("tok", [P, N, H])
        n_tok = sb("n_tok", [P, 2, G, H])
        x1T = sb("x1T", [P, G + N, S])

        w_in = sb("w_in", [P, 4, H])
        w_first = sb("w_first", [P, 2, G, H])
        w_last = sb("w_last", [P, BR, H])
        w_mid = sb("w_mid", [P, 2, H])
        gb0_row = sb("gb0_row", [P, 2, H])
        cols0 = sb("cols0", [P, 7])
        SR_HI, MID, GAMMA, BETA = range(3, 7)
        b_last = sb("b_last", [P, BR, H])
        wi_sb = sb("wi_sb", [P, E, I])
        wo_sb = sb("wo_sb", [P, E, KI, H])
        b_hid = sb("b_hid", [P, E, KI])
        w_hid = sb("w_hid", [P, 4, I])
        bo_row = sb("bo_row", [P, E, H])
        g1_row = sb("g1_row", [P, E, H])
        be1_row = sb("be1_row", [P, E, H])

        xT = sb("xT", [P, G, S])
        h_lo = sb("h_lo", [P, 2, G, S])
        h_hi = sb("h_hi", [P, G, S])
        h_sr = sb("h_sr", [P, G, S])
        hidT = sb("hidT", [P, 2, KI, S])
        stats0 = sb("stats0", [P, G, 6])
        mv0 = sb("mv0", [P, 2, G, 2])
        var0 = sb("var0", [P, 2, G])
        rstd0 = sb("rstd0", [P, 2, G])
        stats1 = sb("stats1", [P, 2, 6])
        mv1 = sb("mv1", [P, 2, 2, 2])
        var1 = sb("var1", [P, 2, 2])
        rstd1 = sb("rstd1", [P, 2, 2])
        eps0 = sb("eps0", [P, G])
        eps1 = sb("eps1", [P, 2])
        gelu_fetched = sb("gelu_fetched", [P, 1])
        minus_half = sb("minus_half", [P, G])

        p_xT = psum("p_xT", [P, G, S])
        p_hT = [psum(f"p_hT{k}", [P, G, S]) for k in range(2)]
        p_mid = psum("p_mid", [P, G, S])
        p_last = psum("p_last", [P, G, H])
        p_x1T = psum("p_x1T", [P, G, S])
        p_hid = [psum(f"p_hid{k}", [P, I]) for k in range(2)]
        p_out = (p_mid, p_xT)
        p_out_last = p_last

        idx_loaded = sem("idx_loaded")
        x_loaded = [sem(f"x_loaded{k}") for k in range(2)]
        tok_start_loaded = sem("tok_start_loaded")
        tok_rest_loaded = sem("tok_rest_loaded")
        w_in_loaded = sem("w_in_loaded")
        cols0_loaded = sem("cols0_loaded")
        b_last_loaded = sem("b_last_loaded")
        b_hid_loaded = sem("b_hid_loaded")
        w0_loaded = sem("w0_loaded")
        wi_loaded = sem("wi_loaded")
        wo_loaded = sem("wo_loaded")
        bo_loaded = sem("bo_loaded")
        rows_loaded = sem("rows_loaded")
        zeroed = sem("zeroed")
        ident_made = sem("ident_made")
        idx_step = sem("idx_step")
        idx_ready = sem("idx_ready")
        psum_cleared = sem("psum_cleared")
        xT_done = sem("xT_done")
        xT_copied = sem("xT_copied")
        w_first_ready = sem("w_first_ready")
        lo_done = sem("lo_done")
        hi_done = sem("hi_done")
        h_ready = sem("h_ready")
        last_mid_done = sem("last_mid_done")
        sr_ready = sem("sr_ready")
        mask_ready = sem("mask_ready")
        selected = sem("selected")
        last_done = sem("last_done")
        xb_ready = sem("xb_ready")
        y_ready = sem("y_ready")
        stats0_ready = sem("stats0_ready")
        mv0_ready = sem("mv0_ready")
        var0_ready = sem("var0_ready")
        rstd0_ready = sem("rstd0_ready")
        n_ready = sem("n_ready")
        residual_ready = sem("residual_ready")
        x1T_done = sem("x1T_done")
        x1T_copied = sem("x1T_copied")
        bo_ready = sem("bo_ready")
        biased = sem("biased")
        w_hid_ready = sem("w_hid_ready")
        hid_done = sem("hid_done")
        hidT_ready = sem("hidT_ready")
        o_done = sem("o_done")
        r_ready = sem("r_ready")
        stats1_ready = sem("stats1_ready")
        mv1_ready = sem("mv1_ready")
        var1_ready = sem("var1_ready")
        rstd1_ready = sem("rstd1_ready")
        centred = sem("centred")
        y1_ready = sem("y1_ready")
        stored = sem("stored")
        sp_passed = sem("sp_passed")
        dve_passed = sem("dve_passed")

        x_dram = x.rearrange("(g j) s h -> g s j h", j=G)
        out_dram = out.rearrange("(g j) s h -> g s j h", j=G)

        def wait_alone(eng, s, value, passed):
            eng.wait_ge(s, value)
            eng.sem_inc(passed, 1)

        def group(t, g):
            return t[:, bass.ds(g * G, G), :]

        registers = {}

        def load_values(eng, name, src, first, count, top):
            for k in range(count):
                if f"{name}{k}" not in registers:
                    registers[f"{name}{k}"] = eng.alloc_register(f"{name}{k}")
            regs = [registers[f"{name}{k}"] for k in range(count)]
            eng.load(regs, src[0:1, bass.ds(first, count)])
            return regs, lambda k: eng.snap(regs[k], min_val=0, max_val=top)

        block = ctx.enter_context(nc.Block())

        def row(ap, first, n, parts=P):
            return ap[first:first + n].rearrange("(a n) -> a n", a=1).broadcast_to([parts, n])

        def flat(t):
            return t.rearrange("p a h -> p (a h)")

        W0 = 3 * 16
        ROWS = 2 * 16
        ZEROED = 6
        FIRST, LAST = 3, NG - 2

        @block.sync
        def _(sp):
            def load_x(g, par):
                if g > 1:
                    sp.wait_ge(xT_done, g - 1)
                sp.dma_start(x_in[:, par], x_dram[g]).then_inc(x_loaded[par], 16)

            def token_major(first, count):
                return x[first * G:(first + count) * G].rearrange("n s h -> s n h")

            load_x(0, 0)
            sp.dma_start(flat(w_in[:]), w0[:, 0:4 * H]).then_inc(w_in_loaded, 16)
            load_x(1, 1)
            sp.dma_start(flat(w_mid[:]), w0[:, 7 * H:9 * H]).then_inc(w0_loaded, 16)
            sp.dma_start(flat(b_last[:, 0:3, :]), row(rows0, 0, 3 * H)).then_inc(b_last_loaded, 16)
            sp.dma_start(flat(w_last[:, 0:3, :]), w0[:, 4 * H:7 * H]).then_inc(w0_loaded, 16)
            sp.dma_start(tok[:, 0:2 * G, :], token_major(0, 2)).then_inc(tok_start_loaded, 16)
            sp.dma_start(flat(gb0_row[:]), row(rows0, 3 * H, 2 * H)).then_inc(w0_loaded, 16)
            sp.dma_start(b_hid[:], b_hid_dram).then_inc(b_hid_loaded, 16)
            load_x(2, 0)
            load_x(3, 1)
            sp.dma_start(tok[:, 2 * G:N, :], token_major(2, NG - 2)).then_inc(tok_rest_loaded, 16)
            sp.dma_start(flat(bo_row[:]), row(rows1, 0, E * H)).then_inc(bo_loaded, 16)
            load_x(4, 0)
            load_x(5, 1)
            sp.dma_start(wi_sb[:], wi).then_inc(wi_loaded, 16)
            for g in range(6, NG):
                load_x(g, g % 2)
            sp.dma_start(wo_sb[:], wo).then_inc(wo_loaded, 16)
            for k, t in enumerate((g1_row, be1_row)):
                sp.dma_start(flat(t[:]), row(rows1, (k + 1) * E * H, E * H)).then_inc(rows_loaded, 16)

            with sp.Fori(0, NG - 1) as g:
                wait_alone(sp, y1_ready, g * G + G, sp_passed)
                sp.dma_start(out_dram[bass.ds(g, 1)].rearrange("a s j h -> (a s) j h"),
                             group(tok, g)).then_inc(stored, 16)
            for first in (N - G, N - G + 2):
                sp.wait_ge(y1_ready, first + 2)
                sp.dma_start(out[first:first + 2].rearrange("n s h -> s n h"), tok[:, first:first + 2, :]).then_inc(stored, 16)
            sp.wait_ge(stored, 16 * (NG + 1))

        @block.gpsimd
        def _(pool):
            nc.gpsimd.memset(ident[:], 0.0).then_inc(zeroed, 1)
            pool.wait_ge(zeroed, 1)
            nc.gpsimd.affine_select(out=ident[:], in_=ident[:], compare_op=ALU.not_equal, fill=1.0, base=0,
                                    pattern=[[-1, P]], channel_multiplier=1).then_inc(ident_made, 1)
            nc.gpsimd.memset(b_last[:, 3, :], 0.0).then_inc(zeroed, 1)
            nc.gpsimd.memset(w_last[:, 3, :], 0.0).then_inc(zeroed, 1)
            nc.gpsimd.memset(minus_half[:], -0.5).then_inc(zeroed, 1)
            nc.gpsimd.memset(eps0[:], EPS0).then_inc(zeroed, 1)
            nc.gpsimd.memset(eps1[:], EPS1).then_inc(zeroed, 1)
            nc.gpsimd.memset(n_tok[:, 1], 0.0).then_inc(n_ready, G)
            pool.wait_ge(zeroed, ZEROED)

            def add_last_bias(g):
                _, br = load_values(pool, "pool_br", branch, g * G, G, BR - 1)
                for j in range(G):
                    at = tok[:, bass.ds(g * G + j, 1), :]
                    nc.gpsimd.tensor_tensor(out=at, in0=at, in1=b_last[:, bass.ds(br(j), 1), :], op=ALU.add).then_inc(xb_ready, 1)

            def invert_deviation0(g, par):
                pool.wait_ge(mv0_ready, g * G + G)
                nc.gpsimd.tensor_tensor(out=var0[:, par, :], in0=mv0[:, par, :, 1], in1=eps0[:], op=ALU.add).then_inc(var0_ready, 1)
                pool.wait_ge(var0_ready, g + 1)
                nc.gpsimd.tensor_tensor(out=rstd0[:, par, :], in0=var0[:, par, :], in1=minus_half[:], op=ALU.pow).then_inc(rstd0_ready, 1)

            def residual(g, par):
                pool.wait_ge(n_ready, g * G + 2 * G)
                nc.gpsimd.tensor_tensor(out=group(tok, g), in0=n_tok[:, par],
                                        in1=gb0_row[:, 0:1, :].broadcast_to([P, G, H]), op=ALU.mult).then_inc(residual_ready, 1)

            def add_bo(i, e):
                nc.gpsimd.tensor_tensor(out=tok[:, bass.ds(i, 1), :], in0=tok[:, bass.ds(i, 1), :],
                                        in1=bo_row[:, bass.ds(e, 1), :], op=ALU.add).then_inc(biased, 1)

            def invert_deviation1(u, par):
                if not isinstance(u, int) or u > 1:
                    pool.wait_ge(y1_ready, 2 * u - 2)
                pool.wait_ge(mv1_ready, 2 * u + 2)
                nc.gpsimd.tensor_tensor(out=var1[:, par, :], in0=mv1[:, par, :, 1], in1=eps1[:], op=ALU.add).then_inc(var1_ready, 1)
                pool.wait_ge(var1_ready, u + 1)
                nc.gpsimd.tensor_tensor(out=rstd1[:, par, :], in0=var1[:, par, :], in1=minus_half[:, 0:2], op=ALU.pow).then_inc(rstd1_ready, 1)

            def step(g, par):
                if not isinstance(g, int) or g < NG - 1:
                    add_last_bias(g + 1)
                invert_deviation0(g, par)
                residual(g - 1, 1 - par)

            pool.wait_ge(idx_ready, 1)
            pool.wait_ge(b_last_loaded, 16)
            pool.wait_ge(tok_start_loaded, 16)
            add_last_bias(0)
            add_last_bias(1)
            pool.wait_ge(tok_rest_loaded, 16)
            invert_deviation0(0, 0)
            pool.wait_ge(w0_loaded, W0)
            step(1, 1)
            pool.wait_ge(bo_loaded, 16)
            nc.gpsimd.tensor_tensor(out=bo_row[:], in0=bo_row[:], in1=gb0_row[:, 1:2, :].broadcast_to([P, E, H]),
                                    op=ALU.add).then_inc(bo_ready, 1)
            step(2, 0)
            with pool.Fori(FIRST, LAST, 2) as g:
                step(g, 1)
                step(g + 1, 0)
            pool.wait_ge(residual_ready, 2)
            pool.wait_ge(bo_ready, 1)

            def group_step(q, first=False):
                _, ex = load_values(pool, "pool_ex", expert_of, q * G, G, E - 1)
                for j in range(G):
                    add_bo(q * G + j, ex(j))
                    if j % 2 == 1 and not first:
                        invert_deviation1(2 * q - 4 + j // 2, j // 2)

            group_step(0, True)
            step(NG - 1, 1)
            residual(NG - 1, 1)
            group_step(1, True)
            group_step(2)
            pool.wait_ge(residual_ready, NG)
            with pool.Fori(3, NG) as q:
                group_step(q)
            for u in range(2 * NG - 4, 2 * NG):
                invert_deviation1(u, u % 2)

        @block.tensor
        def _(pe):
            def transpose_x(g, par):
                pe.wait_ge(x_loaded[par], 8 * (g - par) + 16)
                for j in range(G):
                    mm = nc.tensor.transpose(p_xT[:, j, :], x_in[:, par, j, :], ident[:])
                mm.then_inc(xT_done, 1)

            def transpose_n(g, par):
                pe.wait_ge(n_ready, g * G + 2 * G)
                if isinstance(g, int) and g >= NG - 4:
                    pe.wait_ge(x1T_copied, g + 1)
                for j in range(G):
                    mm = nc.tensor.transpose(p_x1T[:, j, :], n_tok[:, par, j, :], ident[:])
                mm.then_inc(x1T_done, 1)

            def load_branches(g, par):
                return load_values(pe, f"pe_br{par}_", branch, g * G, G, BR - 1)

            def first_product(g, par):
                if not isinstance(g, int) or g > 0:
                    pe.wait_ge(w_first_ready, g * G + G)
                pe.wait_ge(xT_copied, g + 1)
                for j in range(G):
                    if isinstance(g, int) and g == 0:
                        pe.wait_ge(w_first_ready, j + 1)
                    mm = nc.tensor.matmul(p_hT[0][:, j, :], w_first[:, par, j, :], xT[:, j, :], start=True, stop=True)
                    mm.then_inc(lo_done, 1)
                nc.tensor.matmul(flat(p_hT[1][:]), w_in[:, 3, :], flat(xT[:]), start=True, stop=True).then_inc(hi_done, 1)

            def mid_product(g, par, c):
                for j in range(G):
                    with pe.If_eq(c[j], SR):
                        pe.wait_ge(h_ready, (G + 1) * (g + 1))
                        nc.tensor.matmul(p_mid[:, j, :], w_mid[:, 0, :], h_lo[:, par, j, :], start=True, stop=False)
                        nc.tensor.matmul(p_mid[:, j, :], w_mid[:, 1, :], h_hi[:, j, :], start=False, stop=True)

            def last_product(g, par, c):
                weights = [flat(w_last[:, bass.ds(pe.snap(c[j], min_val=0, max_val=BR - 1), 1), :]) for j in range(G)]
                pe.wait_ge(selected, g + 1)
                for j in range(G):
                    mm = nc.tensor.matmul(p_last[:, j, :], h_lo[:, par, j, :], weights[j], start=True, stop=True)
                mm.then_inc(last_done, 1)

            def step(g, par, back=True):
                before = branches[1 - par]
                mid_product(g - 1, 1 - par, before)
                first_product(g, par)
                if not isinstance(g, int) or g < NG - 1:
                    transpose_x(g + 1, 1 - par)
                load_branches(g, par)
                if back:
                    transpose_n(g - 4, par)
                last_product(g - 1, 1 - par, before)

            def keep_warm(count):
                for _ in range(count):
                    nc.tensor.transpose(p_x1T[:, 0, :], ident[:], ident[:])

            pe.wait_ge(ident_made, 1)
            keep_warm(9)
            transpose_x(0, 0)
            keep_warm(5)
            pe.wait_ge(w_in_loaded, 16)
            first_product(0, 0)
            transpose_x(1, 1)
            pe.wait_ge(idx_ready, 1)
            branches = [load_branches(g, g)[0] for g in range(2)]
            pe.wait_ge(w0_loaded, W0)
            pe.wait_ge(psum_cleared, 1)
            pe.wait_ge(zeroed, ZEROED)
            step(1, 1, False)
            step(2, 0, False)
            with pe.Fori(FIRST, LAST, 2) as g:
                step(g, 1)
                step(g + 1, 0)
            step(NG - 1, 1)

            def hidden(i, slot, par, after_mid=False):
                pe.wait_ge(w_hid_ready, i + 1)
                for k in range(KI):
                    cols = slice(k * P, (k + 1) * P)
                    mm = nc.tensor.matmul(p_hid[par][:, cols], w_hid[:, slot, cols], flat(x1T[:, bass.ds(G + i, 1), :]),
                                          start=True, stop=True)
                    if k == 0 and after_mid:
                        mm.then_inc(last_mid_done, 1)
                mm.then_inc(hid_done, 1)

            def output(i, j, e, last=False):
                out_at = p_out_last[:, 0, :] if last else p_out[j // 2][:, j % 2, :]
                for k in range(KI):
                    if k % 2 == 0:
                        pe.wait_ge(hidT_ready, KI * i + k + 2)
                    mm = nc.tensor.matmul(out_at, hidT[:, j % 2, k, :],
                                          wo_sb[:, bass.ds(e, 1), k, :].rearrange("p a h -> p (a h)"),
                                          start=(k == 0), stop=(k == KI - 1))
                mm.then_inc(o_done, 1)

            mid_product(NG - 1, 1, branches[1])
            hidden(0, 0, 0, after_mid=True)
            hidden(1, 1, 1)
            transpose_n(NG - 4, 0)
            last_product(NG - 1, 1, branches[1])
            _, e0 = load_values(pe, "pe_e0_", expert_of, 0, G - 1, E - 1)
            pe.wait_ge(wo_loaded, 16)

            def group_step(q, first=False, last=False):
                for j in range(G):
                    i = q * G + j
                    if j == G - 1 and not first and not last:
                        pe.wait_ge(x1T_copied, NG + 1)
                    if j < G - 1 + (not last) and not (first and j == 0):
                        hidden(i + 1, (j + 1) % 4, (j + 1) % 2)
                    if first and j > 0:
                        transpose_n(NG - G + j, j % 2)
                    if j % 2 == 0 and not first:
                        pe.wait_ge(r_ready, 2 * q + j // 2 - 1)
                    if j == G - 1:
                        load_values(pe, "pe_ex", expert_of, i, 1 if last else G, E - 1)
                    output(i, j, e0(j) if first and j < G - 1 else pe.snap(registers[f"pe_ex{(j + 1) % G}"], min_val=0, max_val=E - 1),
                           last=last and j == G - 1)

            group_step(0, first=True)
            with pe.Fori(1, NG - 1) as q:
                group_step(q)
            group_step(NG - 1, last=True)

        @block.scalar
        def _(act):
            act.dma_start(flat(raw_idx[:]), indices.rearrange("(a b) n -> a (b n)", a=1).broadcast_to([P, 2 * N])).then_inc(idx_loaded, 16)
            act.dma_start(cols0[:], cols0_dram).then_inc(cols0_loaded, 16)
            act.wait_ge(zeroed, ZEROED)
            nc.scalar.activation(gelu_fetched[:], eps0[:, 0:1], ACT.Gelu)

            def copy_xT(g):
                act.wait_ge(xT_done, g + 1)
                nc.scalar.copy(xT[:], p_xT[:]).then_inc(xT_copied, 1)

            def gelu_in(g, par):
                _, br = load_values(act, "act_br", branch, g * G, G, BR - 1)
                act.wait_ge(lo_done, g * G + G)
                for j in range(G):
                    nc.scalar.activation(h_lo[:, par, j:j + 1, :], p_hT[0][:, j:j + 1, :], ACT.Gelu,
                                         bias=cols0[:, bass.ds(br(j), 1)]).then_inc(h_ready, 1)
                act.wait_ge(hi_done, g + 1)
                nc.scalar.activation(h_hi[:], p_hT[1][:], ACT.Gelu, bias=cols0[:, SR_HI:SR_HI + 1]).then_inc(h_ready, 1)

            def gelu_mid(g):
                if isinstance(g, int) and g == NG - 1:
                    act.wait_ge(last_mid_done, 1)
                else:
                    act.wait_ge(lo_done, g * G + G + 1)
                nc.scalar.activation(h_sr[:], p_mid[:], ACT.Gelu, bias=cols0[:, MID:MID + 1]).then_inc(sr_ready, 1)

            def copy_x1T(g):
                act.wait_ge(x1T_done, g + 2)
                nc.scalar.activation(group(x1T, g + 1), p_x1T[:], ACT.Identity, bias=cols0[:, BETA:BETA + 1],
                                     scale=cols0[:, GAMMA:GAMMA + 1]).then_inc(x1T_copied, 1)

            def step(g, par, back=True):
                gelu_mid(g - 1)
                gelu_in(g, par)
                if back:
                    copy_x1T(g - 4)
                copy_xT(g + 1)

            copy_xT(0)
            act.wait_ge(idx_ready, 1)
            act.wait_ge(cols0_loaded, 16)
            gelu_in(0, 0)
            copy_xT(1)
            step(1, 1, False)
            step(2, 0, False)
            with act.Fori(FIRST, LAST, 2) as g:
                step(g, 1)
                step(g + 1, 0)
            _, ex = load_values(act, "act_e0_", expert_of, 0, G, E - 1)

            def place_w_hid(i):
                nc.scalar.copy(w_hid[:, i:i + 1, :], wi_sb[:, bass.ds(ex(i), 1), :]).then_inc(w_hid_ready, 1)

            gelu_mid(NG - 2)
            gelu_in(NG - 1, 1)
            act.wait_ge(wi_loaded, 16)
            place_w_hid(0)
            place_w_hid(1)
            copy_x1T(NG - 5)
            gelu_mid(NG - 1)
            place_w_hid(2)
            place_w_hid(3)

            act.wait_ge(b_hid_loaded, 16)

            def gelu_hidden(i, par, e):
                act.wait_ge(hid_done, i + 1)
                for k in range(KI):
                    nc.scalar.activation(hidT[:, par, k, :], p_hid[par][:, k * P:(k + 1) * P], ACT.Gelu,
                                         bias=b_hid[:, bass.ds(e, 1), k]).then_inc(hidT_ready, 1)

            def group_step(q, first=False):
                _, ex = load_values(act, "act_ex", expert_of, q * G, G, E - 1)
                for j in range(G):
                    gelu_hidden(q * G + j, j % 2, ex(j))
                    if first:
                        copy_x1T(NG - G + j)

            group_step(0, first=True)
            with act.Fori(1, NG) as q:
                group_step(q)

        @block.vector
        def _(dve):
            dve.wait_ge(idx_loaded, 16)
            nc.vector.tensor_scalar(idx_tmp[:, 0, :], raw_idx[0:1, 0, :], 0, 8, ALU.is_lt, ALU.mult).then_inc(idx_step, 1)
            nc.vector.tensor_scalar(idx_tmp[:, 1, :], raw_idx[0:1, 1, :], 0, E, ALU.is_lt, ALU.mult).then_inc(idx_step, 1)
            nc.vector.memset(branch[:, N:N + 2 * G], 0).then_inc(idx_step, 1)
            dve.wait_ge(idx_step, 3)
            nc.vector.tensor_tensor(branch[:, 0:N], raw_idx[0:1, 0, :], idx_tmp[:, 0, :], ALU.max).then_inc(idx_step, 1)
            nc.vector.tensor_tensor(expert_of[:], raw_idx[0:1, 1, :], idx_tmp[:, 1, :], ALU.add).then_inc(idx_step, 1)
            dve.wait_ge(idx_step, 5)
            nc.vector.tensor_scalar(branch[:, 0:N], branch[:, 0:N], 3, None, ALU.min).then_inc(idx_step, 1)
            nc.vector.tensor_scalar(expert_of[:], expert_of[:], 0, E - 1, ALU.max, ALU.min).then_inc(idx_step, 1)
            dve.wait_ge(idx_step, 7)
            nc.vector.nop().then_inc(idx_ready, 1)

            def place_w_first(g, par):
                _, br = load_values(dve, "dve_br", branch, g * G, G, BR - 1)
                for j in range(G):
                    nc.vector.tensor_copy(w_first[:, par, j:j + 1, :], w_in[:, bass.ds(br(j), 1), :]).then_inc(w_first_ready, 1)

            dve.wait_ge(w_in_loaded, 16)
            place_w_first(0, 0)
            nc.vector.memset(p_mid[:], 0.0).then_inc(psum_cleared, 1)
            place_w_first(1, 1)
            nc.vector.tensor_scalar(is_sr[:, 0:N], raw_idx[:, 0, :], SR, None, ALU.is_equal).then_inc(idx_step, 1)
            nc.vector.memset(is_sr[:, N:N + G], 0).then_inc(idx_step, 1)
            dve.wait_ge(idx_step, 9)

            def select(g, par):
                wait_alone(dve, sr_ready, g + 1, dve_passed)
                nc.vector.copy_predicated(h_lo[:, par], sr_mask[:, :, None].broadcast_to([P, G, S]), h_sr[:]).then_inc(selected, 1)

            def set_mask(g):
                if not isinstance(g, int) or g > 0:
                    dve.wait_ge(selected, g)
                nc.vector.tensor_copy(sr_mask[:], is_sr[:, bass.ds(g * G, G)]).then_inc(mask_ready, 1)

            def norm0(g, par):
                dve.wait_ge(rstd0_ready, g + 1)
                for j in range(G):
                    nc.vector.tensor_scalar(n_tok[:, par, j:j + 1, :], tok[:, bass.ds(g * G + j, 1), :],
                                            mv0[:, par, j, 0:1], rstd0[:, par, j:j + 1],
                                            ALU.subtract, ALU.mult).then_inc(n_ready, 1)

            def step(g, par):
                dve.wait_ge(last_done, g + 1)
                dve.wait_ge(xb_ready, g * G + G)
                nc.vector.tensor_tensor(group(tok, g), p_last[:], group(tok, g), ALU.add).then_inc(y_ready, 1)
                wait_alone(dve, y_ready, g + 1, dve_passed)
                for j in range(G):
                    nc.vector.bn_stats(stats0[:, j, :], flat(tok[:, bass.ds(g * G + j, 1), :])).then_inc(stats0_ready, 1)
                if not isinstance(g, int) or g < NG - 1:
                    dve.wait_ge(mask_ready, g + 2)
                    select(g + 1, 1 - par)
                wait_alone(dve, stats0_ready, g * G + G, dve_passed)
                for j in range(G):
                    nc.vector.bn_aggr(mv0[:, par, j, :], stats0[:, j, :]).then_inc(mv0_ready, 1)
                if not isinstance(g, int) or g > 0:
                    norm0(g - 1, 1 - par)
                if not isinstance(g, int) or g < NG - 2:
                    set_mask(g + 2)
                if not isinstance(g, int) or g + 3 < NG:
                    place_w_first(g + 3, 1 - par)

            def place_w_hid(i, slot, e):
                if not isinstance(i, int) or i > 3:
                    dve.wait_ge(hid_done, i - 3)
                nc.vector.tensor_copy(w_hid[:, slot:slot + 1, :], wi_sb[:, bass.ds(e, 1), :]).then_inc(w_hid_ready, 1)

            dve.wait_ge(lo_done, G)
            place_w_first(2, 0)
            set_mask(0)
            dve.wait_ge(mask_ready, 1)
            select(0, 0)
            set_mask(1)
            for g in range(FIRST):
                step(g, g % 2)
            with dve.Fori(FIRST, LAST, 2) as g:
                step(g, 1)
                step(g + 1, 0)
            step(NG - 1, 1)

            def pair_step(u, par, before=None, then=()):
                pair = tok[:, bass.ds(u * 2, 2), :]
                dve.wait_ge(o_done, 2 * u + 2)
                dve.wait_ge(biased, 2 * u + 2)
                nc.vector.tensor_tensor(pair, p_out[par][:, 0:2, :], pair, ALU.add).then_inc(r_ready, 1)
                if before is not None:
                    dve.wait_ge(mv1_ready, 2 * u)
                    centre(u - 1, 1 - par, before)
                for args in then[0:1]:
                    place_w_hid(*args)
                wait_alone(dve, r_ready, u + 1, dve_passed)
                for j in range(2):
                    nc.vector.bn_stats(stats1[:, j, :], flat(tok[:, bass.ds(2 * u + j, 1), :])).then_inc(stats1_ready, 1)
                for args in then[1:2]:
                    place_w_hid(*args)
                wait_alone(dve, stats1_ready, 2 * u + 2, dve_passed)
                for j in range(2):
                    nc.vector.bn_aggr(mv1[:, par, j, :], stats1[:, j, :]).then_inc(mv1_ready, 1)
                if before is not None:
                    scale(u - 1, 1 - par, before)

            def centre(u, par, e):
                for j in range(2):
                    rj = tok[:, bass.ds(2 * u + j, 1), :]
                    nc.vector.scalar_tensor_tensor(out=rj, in0=rj, scalar=mv1[:, par, j, 0:1],
                                                   in1=g1_row[:, bass.ds(e[j], 1), :],
                                                   op0=ALU.subtract, op1=ALU.mult).then_inc(centred, 1)

            def scale(u, par, e):
                dve.wait_ge(rstd1_ready, u + 1)
                dve.wait_ge(centred, 2 * u + 2)
                for j in range(2):
                    rj = tok[:, bass.ds(2 * u + j, 1), :]
                    nc.vector.scalar_tensor_tensor(out=rj, in0=rj, scalar=rstd1[:, par, j:j + 1],
                                                   in1=be1_row[:, bass.ds(e[j], 1), :],
                                                   op0=ALU.mult, op1=ALU.add).then_inc(y1_ready, 1)

            _, ex = load_values(dve, "dve_ex", expert_of, G, G - 1, E - 1)
            dve.wait_ge(w_hid_ready, G)
            dve.wait_ge(wi_loaded, 16)
            place_w_hid(4, 0, ex(0))
            dve.wait_ge(x1T_done, NG - 1)
            norm0(NG - 1, 1)
            dve.wait_ge(rows_loaded, ROWS)
            pair_step(0, 0, then=((5, 1, ex(1)), (6, 2, ex(2))))

            def group_step(q, last=False):
                n = G + AHEAD + (1 if last else G)
                _, ex = load_values(dve, "dve_ex", expert_of, q * G - G, n, E - 1)
                e = {k - G: ex(k) for k in range(n) if last or k < G or k >= G + AHEAD}
                first = q * G + AHEAD
                pair_step(2 * q - 1, 1, before=(e[-4], e[-3]),
                          then=((first, 3, e[3]),) if last else ((first, 3, e[3]), (first + 1, 0, e[4])))
                pair_step(2 * q, 0, before=(e[-2], e[-1]),
                          then=() if last else ((first + 2, 1, e[5]), (first + 3, 2, e[6])))
                return [e[j] for j in range(G)] if last else None

            with dve.Fori(1, NG - 1) as q:
                group_step(q)
            e = group_step(NG - 1, last=True)
            def add_last(i, src):
                dve.wait_ge(o_done, i + 1)
                dve.wait_ge(biased, i + 1)
                nc.vector.tensor_tensor(tok[:, i, :], src, tok[:, i, :], ALU.add).then_inc(r_ready, 1)

            dve.wait_ge(r_ready, 2 * NG - 1)
            add_last(N - 2, p_out[1][:, 0, :])
            dve.wait_ge(mv1_ready, N - 2)
            centre(2 * NG - 2, 0, e[0:2])
            add_last(N - 1, p_out_last[:, 0, :])
            for j in range(2):
                dve.wait_ge(r_ready, 2 * NG + j)
                nc.vector.bn_stats(stats1[:, j, :], tok[:, N - 2 + j, :]).then_inc(stats1_ready, 1)
            dve.wait_ge(stats1_ready, N)
            for j in range(2):
                nc.vector.bn_aggr(mv1[:, 1, j, :], stats1[:, j, :]).then_inc(mv1_ready, 1)
            scale(2 * NG - 2, 0, e[0:2])
            dve.wait_ge(mv1_ready, N)
            centre(2 * NG - 1, 1, e[2:4])
            scale(2 * NG - 1, 1, e[2:4])


def kernel(**inputs):
    import numpy as _np
    import concourse.bacc as _bacc
    from concourse import mybir as _mybir
    from concourse.bass_utils import run_bass_kernel_spmd as _run

    a0 = {k[len("L0_cond_"):]: _np.asarray(v) for k, v in inputs.items() if k.startswith("L0_cond_")}
    a1 = {k[len("L1_cond_"):]: _np.asarray(v) for k, v in inputs.items() if k.startswith("L1_cond_")}
    h = a0["w1_nr"].shape[0]
    laid_out = {
        "x": _np.asarray(inputs["x"]),
        "indices": _np.stack([_np.asarray(inputs["itok_B_0_2"]), _np.asarray(inputs["itok_B_0_7"])]),
        "w0": _np.concatenate([a0["w1_nr"], a0["w1_tsr"], a0["w1_sr"], a0["w2_nr"], a0["w2_tsr"], a0["w3_sr"],
                               a0["w2_sr"][:h], a0["w2_sr"][h:]], axis=1),
        "rows0": _np.concatenate([a0["b2_nr"], a0["b2_tsr"], a0["b3_sr"], a0["gamma"], a0["beta"]]),
        "cols0": _np.stack([a0["b1_nr"], a0["b1_tsr"], a0["b1_sr"][:h], a0["b1_sr"][h:], a0["b2_sr"],
                            a0["gamma"], a0["beta"]], axis=1),
        "wi": a1["Wi"].transpose(1, 0, 2),
        "wo": a1["Wo"].reshape(a1["Wo"].shape[0], -1, h, h).transpose(2, 0, 1, 3),
        "b_hid": a1["bi"].reshape(-1, a1["bi"].shape[1] // h, h).transpose(2, 0, 1),
        "rows1": _np.concatenate([a1["bo"].ravel(), a1["gamma"].ravel(), a1["beta"].ravel()]),
    }
    nc = _bacc.Bacc("TRN2", target_bir_lowering=False, num_devices=1)
    arrays, args = {}, []
    for name, a in laid_out.items():
        a = _np.ascontiguousarray(a)
        arrays[f"in_{name}_dram"] = a
        args.append(nc.dram_tensor(f"in_{name}_dram", a.shape, _mybir.dt.from_np(a.dtype), kind="ExternalInput").ap())
    args.append(nc.dram_tensor("out_0_dram", laid_out["x"].shape, _mybir.dt.float32, kind="ExternalOutput").ap())
    conditional_then_expert_layers(nc, *args)
    r = _run(nc, [arrays], core_ids=[0])
    return r.results[0]["out_0_dram"]
```
